# Optimizing a Trainium2 kernel written in Bass

```python
import numpy as np
import jax
import jax.numpy as jnp

def _softmax(x, axis=-1):
    return jax.nn.softmax(x, axis=axis)

def _gelu(x):
    return jax.nn.gelu(x, approximate=True)

def _silu(x):
    return jax.nn.silu(x)

def _sigmoid(x):
    return jax.nn.sigmoid(x)

def _layernorm(x, axis=-1, eps=1e-05):
    m = jnp.mean(x, axis=axis, keepdims=True)
    v = jnp.var(x, axis=axis, keepdims=True)
    return (x - m) / jnp.sqrt(v + eps)

def _scatter_add(tgt, idx, src, axis=0):
    return tgt.at[idx].add(src)

def _segment_sum(src, seg, n):
    return jax.ops.segment_sum(src, seg, n)
kernel_name = 'mk_xattn_ffn_d1_seqx_r4_2f1d88'

def setup_inputs(seed: int=0):
    np.random.seed(seed)
    _w = jnp.asarray

    def _rec_inputs():
        import jax
        import jax.numpy as jnp
        _rk = jax.random.key(seed)
        x = -0.0002928 + 1 * jax.random.normal(jax.random.fold_in(_rk, 1), (32, 128, 256), jnp.float32)
        _lenS = 128 - jax.random.randint(jax.random.fold_in(_rk, 7), (32,), 0, max(1, 128 // 4) + 1, jnp.int32)
        _lenS2 = 128 - jax.random.randint(jax.random.fold_in(_rk, 8), (32,), 0, max(1, 128 // 4) + 1, jnp.int32)
        _ctx_1024P = jax.random.normal(jax.random.fold_in(_rk, 11), (32, 16, 256), jnp.float32)
        _ctx_1024c = jax.random.dirichlet(jax.random.fold_in(_rk, 511), 0.3 * jnp.ones((16,), jnp.float32), (32, 128))
        _ctx_1024t = jnp.einsum('bsk,bkd->bsd', _ctx_1024c, _ctx_1024P)
        _ctx_1024t = _ctx_1024t * jax.lax.rsqrt(jnp.mean(jnp.square(_ctx_1024t)) + 1e-12) * 0.953939
        ctx_1024 = -1.39393e-06 + 0.999914 * (_ctx_1024t + 0.3 * jax.random.normal(jax.random.fold_in(_rk, 611), (32, 128, 256), jnp.float32))
        return (x, ctx_1024)
    x, ctx_1024 = _rec_inputs()

    def _L0_xattn_setup():
        import jax, jax.numpy as jnp
        import numpy as np
        HEADS = 16
        key = jax.random.key(seed)
        k1, k2, k3, k4 = jax.random.split(key, 4)
        B, T, S, W = (2, 512, 512, 256)
        x = jax.random.normal(k1, (B, T, W), dtype=jnp.float32)
        cond_k = jax.random.normal(k2, (B, S, W), dtype=jnp.float32)
        cond_v = jax.random.normal(k3, (B, S, W), dtype=jnp.float32)
        w_proj = jax.random.normal(k4, (W, W), dtype=jnp.float32) * 0.02
        b_proj = jnp.zeros((W,), dtype=jnp.float32)
        return {'x': x, 'cond_k': cond_k, 'cond_v': cond_v, 'w_proj': w_proj, 'b_proj': b_proj}
    _L0_xattn_all = _L0_xattn_setup()
    _L0_xattn_in = {k: v for k, v in _L0_xattn_all.items() if k in ('w_proj', 'b_proj')}
    del _L0_xattn_all

    def _L0_ffn_setup():
        import jax, jax.numpy as jnp
        import numpy as np
        D_MODEL, D_FF, N_EXP = (256, 1024, 8)
        key = jax.random.key(seed)
        ks = jax.random.split(key, 8)
        s = lambda fan_in: 1.0 / np.sqrt(fan_in)
        x = jax.random.normal(ks[0], (4, 512, D_MODEL), dtype=jnp.float32)
        Wr = jax.random.uniform(ks[1], (N_EXP, D_MODEL), jnp.float32, -s(D_MODEL), s(D_MODEL))
        br = jax.random.uniform(ks[2], (N_EXP,), jnp.float32, -s(D_MODEL), s(D_MODEL))
        W1 = jax.random.uniform(ks[3], (N_EXP, D_FF, D_MODEL), jnp.float32, -s(D_MODEL), s(D_MODEL))
        b1 = jax.random.uniform(ks[4], (N_EXP, D_FF), jnp.float32, -s(D_MODEL), s(D_MODEL))
        W2 = jax.random.uniform(ks[5], (N_EXP, D_MODEL, D_FF), jnp.float32, -s(D_FF), s(D_FF))
        b2 = jax.random.uniform(ks[6], (N_EXP, D_MODEL), jnp.float32, -s(D_FF), s(D_FF))
        return {'x': x, 'Wr': Wr, 'br': br, 'W1': W1, 'b1': b1, 'W2': W2, 'b2': b2}
    _L0_ffn_all = _L0_ffn_setup()
    _L0_ffn_in = {k: v for k, v in _L0_ffn_all.items() if k in ('Wr', 'br', 'W1', 'b1', 'W2', 'b2')}
    del _L0_ffn_all
    return {'x': x, 'ctx_1024': ctx_1024, 'L0_xattn_w_proj': _L0_xattn_in['w_proj'], 'L0_xattn_b_proj': _L0_xattn_in['b_proj'], 'L0_ffn_Wr': _L0_ffn_in['Wr'], 'L0_ffn_br': _L0_ffn_in['br'], 'L0_ffn_W1': _L0_ffn_in['W1'], 'L0_ffn_b1': _L0_ffn_in['b1'], 'L0_ffn_W2': _L0_ffn_in['W2'], 'L0_ffn_b2': _L0_ffn_in['b2']}

def reference(x, ctx_1024, L0_xattn_w_proj, L0_xattn_b_proj, L0_ffn_Wr, L0_ffn_br, L0_ffn_W1, L0_ffn_b1, L0_ffn_W2, L0_ffn_b2):
    import jax
    import jax.numpy as jnp

    def _L0_xattn_ref(x, cond_k, cond_v, w_proj, b_proj):
        import jax, jax.numpy as jnp
        import numpy as np
        HEADS = 16
        B, T, W = x.shape
        S = cond_k.shape[1]
        H = HEADS
        d = W // H
        scale = 1.0 / jnp.sqrt(jnp.sqrt(jnp.float32(d)))
        q = x.reshape(B, T, H, d) * scale
        k = cond_k.reshape(B, S, H, d) * scale
        v = cond_v.reshape(B, S, H, d)
        scores = jnp.einsum('bthd,bshd->bhts', q, k)
        w = jax.nn.softmax(scores.astype(jnp.float32), axis=-1).astype(scores.dtype)
        out = jnp.einsum('bhts,bshd->bthd', w, v).reshape(B, T, W)
        return out @ w_proj.T + b_proj

    def _L0_ffn_ref(x, Wr, br, W1, b1, W2, b2):
        import jax, jax.numpy as jnp
        import numpy as np
        D_MODEL, D_FF, N_EXP = (256, 1024, 8)
        B, S, D = x.shape
        xf = x.reshape(-1, D)
        logits = xf @ Wr.T + br
        expert_idx = jnp.argmax(logits, axis=-1)
        h = jax.nn.relu(jnp.einsum('td,efd->etf', xf, W1) + b1[:, None, :])
        y = jnp.einsum('etf,edf->etd', h, W2) + b2[:, None, :]
        out = y[expert_idx, jnp.arange(xf.shape[0])]
        return out.reshape(B, S, D)
    x = x + _L0_xattn_ref(_layernorm(x, axis=-1), ctx_1024, ctx_1024, L0_xattn_w_proj, L0_xattn_b_proj)
    x = x + _L0_ffn_ref(_layernorm(x, axis=-1), L0_ffn_Wr, L0_ffn_br, L0_ffn_W1, L0_ffn_b1, L0_ffn_W2, L0_ffn_b2)
    return x

_drawn_inputs = setup_inputs


def setup_inputs(seed=0):
    import zlib

    import numpy as np

    out = dict(_drawn_inputs(seed))
    spreads = {'L0_xattn_b_proj': (0.0, 0.1)}
    factors = {'L0_ffn_b1': 4.106, 'L0_ffn_b2': 3.228}
    for name, (base, spread) in spreads.items():
        noise = np.random.default_rng([zlib.crc32(name.encode()), seed]).standard_normal(out[name].shape)
        drawn = base * np.exp(spread * noise) if base else spread * noise
        out[name] = jnp.asarray(drawn.astype(out[name].dtype))
    for name, factor in factors.items():
        out[name] = (out[name] * factor).astype(out[name].dtype)
    return out
```

```python
from contextlib import ExitStack

import concourse.bass as bass
from concourse import mybir

P = 128
D = 256
H = 16
DH = D // H
PAIRS = H // 2
NB = 32
TOK = NB * P
E = 8
F = 1024
KC = D // P
FC = F // P
TILES = TOK // P + E - 1
REGION = TOK + P
SPARE = E * REGION
ROW = D + 16
NOWHERE = 1.0e6
SCALE = 1.0 / DH ** 0.5
EPS = 1e-5

F32 = mybir.dt.float32
F32R = mybir.dt.float32r
BF16 = mybir.dt.bfloat16
I32 = mybir.dt.int32
U32 = mybir.dt.uint32
ALU = mybir.AluOpType
ACT = mybir.ActivationFunctionType
AX = mybir.AxisListType

CONST_COLS = {}
CONST_WIDTH = 0
for _name, _n in (("ident", P), ("before", P), ("region", E), ("pad_row", E), ("expert", E),
                  ("full_rows", TOK // P), ("tile", TILES), ("tile_row", TILES), ("minus_hi", 1), ("lane", 1), ("power", 1), ("round", 1)):
    CONST_COLS[_name] = (CONST_WIDTH, CONST_WIDTH + _n)
    CONST_WIDTH += _n

RING = (("q_a", -1), ("q_b", -1), ("p0", 0), ("p1", 0), ("o", 1), ("n", 3), ("p2", 0), ("p3", 0))
FIRST_A, LAST_A = -4, NB + 3
LOOP_A = (3, 14)
FIRST_F, LAST_F = -2, TILES + 1
LOOP_F = (2, 18)


def uses_before(step):
    return sum(1 for s in range(FIRST_A, step) for _, lag in RING if 0 <= s - lag < NB)


STEADY = uses_before(2 * LOOP_A[0]) - len(RING) * 2 * LOOP_A[0]


class Step:

    def __init__(self, half, odd, count):
        self.half, self.odd, self.count = half, odd, count
        self.fixed = isinstance(half, int)
        self.number = 2 * half + odd

    def has(self, lag, least=0):
        return not self.fixed or least <= self.number - lag < self.count

    def item(self, lag):
        return self.number - lag

    def side(self, lag):
        return (self.odd - lag) % 2

    def turn(self, lag):
        p = (self.odd - lag) % 2
        return self.half + (self.odd - lag - p) // 2

    def ring(self, name, back=0):
        at = [n for n, _ in RING].index(name)
        if not self.fixed:
            return self.number * len(RING) + (STEADY - back * len(RING) + at)
        s = self.number - back
        return uses_before(s) + sum(1 for _, lag in RING[:at] if 0 <= s - lag < NB)

    def bank(self, name):
        if self.fixed:
            return self.ring(name) % 2
        return (STEADY + [n for n, _ in RING].index(name)) % 2


def walk(engine, first, last, loop, count, body):
    for s in range(first, 2 * loop[0]):
        body(Step(s // 2, s % 2, count))
    with engine.Fori(loop[0], loop[1]) as half:
        body(Step(half, 0, count))
        body(Step(half, 1, count))
    for s in range(2 * loop[1], last + 1):
        body(Step(s // 2, s % 2, count))


def spread(ap, axis, n):
    names = [f"a{i}" for i in range(len(ap.shape))]
    inner = names[:axis] + [f"(o {names[axis]})"] + names[axis + 1:]
    out = names[:axis] + ["o", names[axis]] + names[axis + 1:]
    v = ap.rearrange(" ".join(inner) + " -> " + " ".join(out), o=1)
    shape = list(v.shape)
    shape[axis] = n
    return v.to_broadcast(shape)


def repeat_last(ap, n):
    names = [f"a{i}" for i in range(len(ap.shape))]
    v = ap.rearrange(" ".join(names[:-1] + [f"({names[-1]} o)"]) + " -> " + " ".join(names + ["o"]), o=1)
    return v.to_broadcast(list(ap.shape) + [n])


def build(nc, x, ctx_rows, ctx_heads, w_proj_t, b_proj, wr_t, b_r, experts, b1_cols, b2, consts, out):
    routed = nc.dram_tensor("routed", (SPARE + P, ROW), F32).ap()
    x_rows = x.rearrange("b t d -> (b t) d")
    out_rows = out.rearrange("b t d -> (b t) d")

    with ExitStack() as ctx:
        def sb(name, shape, dt, where=None):
            return (where or ctx).enter_context(nc.sbuf_tensor(name, shape, dt))

        def sem(name):
            return ctx.enter_context(nc.semaphore(name))

        def sems(name):
            return [sem(f"{name}{i}") for i in range(2)]

        psum_s = [ctx.enter_context(nc.psum_tensor(f"scores{h}", [P, PAIRS, P], F32)) for h in range(2)]
        psum_r = [ctx.enter_context(nc.psum_tensor(f"transfer{i}", [P, 512], F32)) for i in range(2)]
        psum_m = [ctx.enter_context(nc.psum_tensor(f"sums{i}", [P, 512], F32)) for i in range(2)]

        cst = sb("cst", [P, CONST_WIDTH], F32)

        def const(name):
            a, b = CONST_COLS[name]
            return cst[:, a:b]

        ident = const("ident")
        before = sb("before", [P, P], BF16)
        ones = sb("ones", [P, P], BF16)
        w_proj_sb = sb("w_proj_sb", [P, KC, D], F32)
        b_proj_sb = sb("b_proj_sb", [P, D], F32)
        wr_sb = sb("wr_sb", [P, KC, E], F32)
        b_r_sb = sb("b_r_sb", [P, E], F32)
        b1_sb = sb("b1_sb", [P, E, FC], F32)
        w_sb = sb("w_sb", [P, 4 * E, F], F32)
        taken = sb("taken", [P, E], BF16)
        pad = sb("pad", [P, ROW], F32)

        consts_in = sem("consts_in")
        consts_set = sem("consts_set")
        experts_in = sem("experts_in")
        spare_written = sem("spare_written")
        x_in, k_in, v_in, xr_in, row_out = sems("x_in"), sems("k_in"), sems("v_in"), sems("xr_in"), sems("row_out")
        stats1, root1, norm1 = sem("stats1"), sem("root1"), sem("norm1")
        q_hi, q_lo = sem("q_hi"), sem("q_lo")
        k_neg, k_ready = sem("k_neg"), sems("k_ready")
        scores_done = [sem("scores_done0"), sem("scores_done1")]
        row_max = sem("row_max")
        shifted_done = [sem("shifted_done0"), sem("shifted_done1")]
        ring_full, ring_read = sem("ring_full"), sem("ring_read")
        v_ready = sem("v_ready")
        pv_done, recip_done, o_done = sem("pv_done"), sem("recip_done"), sem("o_done")
        proj_done, xb_done, x2_done = sem("proj_done"), sem("xb_done"), sem("x2_done")
        stats2, root2, norm2 = sem("stats2"), sem("root2"), sem("norm2")
        logits_done, logits_read = sem("logits_done"), sem("logits_read")
        choice, hot_done = sem("choice"), sem("hot_done")
        rank_done, rank_read, taken_done, place, place_done = (
            sem("rank_done"), sem("rank_read"), sem("taken_done"), sem("place"), sem("place_done"))
        number_set, row_done = sem("number_set"), sem("row_done")

        CONSTS_SET = 5
        CHAIN = 3

        a = ExitStack()
        with a:
            x_sb = [sb(f"x_sb{i}", [P, D], F32, a) for i in range(2)]
            xn = sb("xn", [P, D], F32, a)
            q_parts = sb("q_parts", [P, H, 2, 2, DH], F32, a)
            q_t = sb("q_t", [P, PAIRS, P], F32R, a)
            k_raw = [sb(f"k_raw{i}", [P, PAIRS, P], F32, a) for i in range(2)]
            k_negated = sb("k_negated", [P, PAIRS, P], F32R, a)
            k_t = sb("k_t", [P, PAIRS, 2, P], F32R, a)
            shifted = [sb(f"shifted{i}", [P, PAIRS, P], F32, a) for i in range(2)]
            p_t = sb("p_t", [P, H, P], F32, a)
            v_raw = [sb(f"v_raw{i}", [P, D], F32, a) for i in range(2)]
            v_one = sb("v_one", [P, H, DH + 1], F32, a)
            xr_sb = [sb(f"xr_sb{i}", [P, D], F32, a) for i in range(2)]
            xb = [sb(f"xb{i}", [P, D], F32, a) for i in range(2)]
            o_sb = sb("o_sb", [P, H, DH], F32, a)
            o_t = sb("o_t", [P, KC, P], F32, a)
            x2 = [sb(f"x2{i}", [P, D], F32, a) for i in range(2)]
            row = [sb(f"row{i}", [P, ROW], F32, a) for i in range(2)]
            x2n = sb("x2n", [P, D], F32, a)
            x2n_t = sb("x2n_t", [P, KC, P], F32, a)
            st1, st2 = sb("st1", [P, 6], F32, a), sb("st2", [P, 6], F32, a)
            mv1, mv2 = ([sb(f"mv{n}{i}", [P, 2], F32, a) for i in range(2)] for n in (1, 2))
            ve1, ve2 = ([sb(f"ve{n}{i}", [P, 1], F32, a) for i in range(2)] for n in (1, 2))
            rs1, rs2 = ([sb(f"rs{n}{i}", [P, 1], F32, a) for i in range(2)] for n in (1, 2))
            smax = sb("smax", [P, H], F32, a)
            recip = sb("recip", [P, H], F32, a)
            logits = sb("logits", [P, E], F32, a)
            top = sb("top", [P, E], F32, a)
            top_at = sb("top_at", [P, E], U32, a)
            top_f = sb("top_f", [P, 1], F32, a)
            hot = [sb(f"hot{i}", [P, E], BF16, a) for i in range(2)]
            spot = sb("spot", [P, E], F32, a)
            spot_x = sb("spot_x", [P, E], F32, a)
            spot_f = sb("spot_f", [P, 1], F32, a)
            spot_i = [sb(f"spot_i{i}", [P, 1], U32, a) for i in range(2)]

            block = a.enter_context(nc.Block())

            @block.sync
            def _(sp):
                sp.dma_start(cst[:, :], consts).then_inc(consts_in, 16)
                sp.dma_start(w_proj_sb[:, :, :], w_proj_t.rearrange("(c p) n -> p c n", p=P)).then_inc(consts_in, 16)
                sp.dma_start(wr_sb[:, :, :], wr_t.rearrange("(c p) n -> p c n", p=P)).then_inc(consts_in, 16)
                sp.dma_start(b_proj_sb[:, :], spread(b_proj, 0, P)).then_inc(consts_in, 16)
                sp.dma_start(b_r_sb[:, :], spread(b_r, 0, P)).then_inc(consts_in, 16)
                sp.dma_start(b1_sb[:, :, :], b1_cols).then_inc(consts_in, 16)

                def step(s):
                    if s.has(-4):
                        p = s.side(-4)
                        if s.has(-4, 2):
                            sp.wait_ge(norm1, s.item(-4) - 1)
                        sp.dma_start(x_sb[p][:, :], x_rows[bass.ds(s.item(-4) * P, P), :]).then_inc(x_in[p], 16)
                    if s.has(-2):
                        p = s.side(-2)
                        if s.has(-2, 2):
                            for h in range(2):
                                sp.wait_ge(k_ready[h], s.item(-2) - 1)
                        for h in range(2):
                            sp.dma_start(k_raw[p][64 * h:64 * h + 64, :, :],
                                         spread(ctx_heads[bass.ds(s.item(-2), 1), h].rearrange("b d j s -> (b d) (j s)"), 0, 4)
                                         ).then_inc(k_in[p], 16)
                    if s.has(-1):
                        p = s.side(-1)
                        if s.has(-1, 2):
                            sp.wait_ge(v_ready, s.item(-1) - 1)
                        sp.dma_start(v_raw[p][:, :], ctx_rows[bass.ds(s.item(-1) * P, P), :]).then_inc(v_in[p], 16)
                    if s.has(0):
                        p = s.side(0)
                        if s.has(0, 2):
                            sp.wait_ge(xb_done, s.item(0) - 1)
                        sp.dma_start(xr_sb[p][:, :], x_rows[bass.ds(s.item(0) * P, P), :]).then_inc(xr_in[p], 16)
                        sp.dma_start(w_sb[:, bass.ds(s.item(0), 1), :].rearrange("p c f -> p (c f)"),
                                     experts[bass.ds(s.item(0), 1)].rearrange("c p f -> (c p) f")).then_inc(experts_in, 16)
                walk(sp, FIRST_A, LAST_A, LOOP_A, NB, step)
                sp.wait_ge(consts_set, CONSTS_SET)
                sp.dma_start(routed[SPARE:SPARE + P, :], pad[:, :]).then_inc(spare_written, 16)

            @block.gpsimd
            def _(pool):
                pool.wait_ge(consts_in, 16 * 6)
                pool.memset(pad[:, :], 0.0).then_inc(number_set, 1)
                for p in range(2):
                    pool.memset(row[p][:, D:ROW], 0.0).then_inc(number_set, 1)
                pool.memset(v_one[:, :, DH:DH + 1], 1.0).then_inc(number_set, 1)
                pool.wait_ge(number_set, 4)
                pool.memset(pad[:, D:D + 1], NOWHERE).then_inc(consts_set, 1)
                for p in range(2):
                    pool.tensor_scalar(row[p][:, D:D + 1], const("lane"), float((p - 2) * P), None, ALU.add).then_inc(number_set, 1)

                def step(s):
                    if s.has(-3):
                        p = s.side(-3)
                        pool.wait_ge(stats1, CHAIN * (s.item(-3) + 1))
                        if s.has(-3, 2):
                            pool.wait_ge(norm1, s.item(-3) - 1)
                        pool.tensor_tensor(rs1[p][:, :], ve1[p][:, :], const("power"), ALU.pow).then_inc(root1, 1)
                    if s.has(-2):
                        pool.wait_ge(q_hi, s.item(-2) + 1)
                        for c in range(2):
                            pool.tensor_tensor(q_parts[:, :, c, 1, :], xn[:, :].rearrange("p (h d) -> p h d", h=H),
                                               q_parts[:, :, c, 0, :], ALU.subtract).then_inc(q_lo, 1)
                    if s.has(-1):
                        p = s.side(-1)
                        pool.wait_ge(k_neg, s.item(-1) + 1)
                        pool.wait_ge(k_in[p], 32 * (s.turn(-1) + 1))
                        if s.has(-1, 1):
                            pool.wait_ge(scores_done[1], s.item(-1))
                        else:
                            pool.wait_ge(consts_set, CONSTS_SET)
                        pool.tensor_tensor(k_t[0:64, :, 0, :], k_raw[p][0:64, :, :], k_negated[0:64, :, :].bitcast(F32), ALU.add
                                           ).then_inc(k_ready[0], 1)
                    if s.has(2):
                        p = s.side(2)
                        pool.wait_ge(stats2, CHAIN * (s.item(2) + 1))
                        if s.has(2, 2):
                            pool.wait_ge(norm2, s.item(2) - 1)
                        pool.tensor_tensor(rs2[p][:, :], ve2[p][:, :], const("power"), ALU.pow).then_inc(root2, 1)
                    if s.has(4):
                        p = s.side(4)
                        if s.has(4, 2):
                            pool.wait_ge(row_out[p], 16 * s.turn(4))
                        else:
                            pool.wait_ge(number_set, 5 + p)
                        pool.tensor_tensor(row[p][:, D:D + 1], row[p][:, D:D + 1], const("round"), ALU.add).then_inc(number_set, 1)
                        pool.wait_ge(number_set, 7 + s.item(4))
                        pool.wait_ge(row_done, s.item(4) + 1)
                        pool.wait_ge(place_done, s.item(4) + 1)
                    if s.has(1):
                        p1 = s.side(1)
                        pool.wait_ge(xr_in[p1], 16 * (s.turn(1) + 1))
                        if s.has(1, 2):
                            pool.wait_ge(x2_done, s.item(1) - 1)
                        pool.tensor_tensor(xb[p1][:, :], xr_sb[p1][:, :], b_proj_sb[:, :], ALU.add).then_inc(xb_done, 1)
                    if s.has(4):
                        pool.indirect_dma_start(
                            out=routed, out_offset=bass.IndirectOffsetOnAxis(ap=spot_i[p][:, 0:1], axis=0),
                            in_=row[p][:, :], in_offset=None).then_inc(row_out[p], 16)
                walk(pool, FIRST_A, LAST_A, LOOP_A, NB, step)
                for p in range(2):
                    pool.wait_ge(row_out[p], 16 * (NB // 2))
                pool.wait_ge(spare_written, 16)

            @block.scalar
            def _(act):
                act.wait_ge(consts_in, 16 * 6)

                def read_ring(s, name, out, func, scale=1.0):
                    n = s.ring(name)
                    act.wait_ge(ring_full, n + 1)
                    src = psum_r[s.bank(name)][:, 0:out.free_size()]
                    if len(out.shape) == 3:
                        src = src.rearrange("p (c t) -> p c t", c=out.shape[1])
                    act.activation(out, src, func, scale=scale).then_inc(ring_read, 1)

                def step(s):
                    if s.has(-1):
                        p = s.side(-1)
                        act.wait_ge(k_in[p], 32 * (s.turn(-1) + 1))
                        if s.has(-1, 1):
                            for h in range(2):
                                act.wait_ge(k_ready[h], s.item(-1))
                        act.activation(k_negated[:, :, :], k_raw[p][:, :, :], ACT.Copy, scale=const("minus_hi")).then_inc(k_neg, 1)
                        for n, name in enumerate(("q_a", "q_b")):
                            if n == 0 and s.has(-1, 1):
                                act.wait_ge(scores_done[1], s.item(-1))
                            read_ring(s, name, q_t[:, 4 * n:4 * n + 4, :], ACT.Copy)
                    if s.has(0):
                        p = s.side(0)
                        act.wait_ge(v_in[p], 16 * (s.turn(0) + 1))
                        if s.has(0, 1):
                            act.wait_ge(pv_done, s.item(0))
                        act.activation(v_one[:, :, 0:DH], v_raw[p][:, :].rearrange("p (h d) -> p h d", h=H), ACT.Copy).then_inc(v_ready, 1)
                        for n in range(2):
                            read_ring(s, f"p{n}", p_t[:, 4 * n:4 * n + 4, :], ACT.Exp, scale=SCALE)
                    if s.has(1):
                        if s.has(1, 1):
                            act.wait_ge(proj_done, s.item(1))
                        read_ring(s, "o", o_t[:, :, :], ACT.Copy)
                    if s.has(3):
                        p = s.side(3)
                        act.wait_ge(x2_done, s.item(3) + 1)
                        if s.has(3, 2):
                            act.wait_ge(row_out[p], 16 * s.turn(3))
                        act.activation(row[p][:, 0:D], x2[p][:, :], ACT.Copy).then_inc(row_done, 1)
                        if s.has(3, 1):
                            act.wait_ge(logits_done, s.item(3))
                        read_ring(s, "n", x2n_t[:, :, :], ACT.Copy)
                    if s.has(0):
                        for n in range(2, 4):
                            read_ring(s, f"p{n}", p_t[:, 4 * n:4 * n + 4, :], ACT.Exp, scale=SCALE)
                walk(act, FIRST_A, LAST_A, LOOP_A, NB, step)

            @block.tensor
            def _(pe):
                pe.wait_ge(consts_in, 16 * 6)
                pe.wait_ge(consts_set, CONSTS_SET)

                def transposes(s, name, parts):
                    n = s.ring(name)
                    if not s.fixed or n >= 2:
                        pe.wait_ge(ring_read, n - 1)
                    for c, part in enumerate(parts):
                        last = pe.transpose(psum_r[s.bank(name)][:, P * c:P * c + P], part, ident)
                    last.then_inc(ring_full, 1)

                def step(s):
                    if s.has(0):
                        b = s.item(0)
                        pe.wait_ge(ring_read, s.ring("q_b", 1) + 1)
                        for h in range(2):
                            pe.wait_ge(k_ready[h], b + 1)
                        for half in range(2):
                            if s.has(0, 1):
                                pe.wait_ge(shifted_done[half], b)
                            for j in range(PAIRS // 2):
                                pair = PAIRS // 2 * half + j
                                last = pe.matmul(psum_s[half][:, 2 * j:2 * j + 2, :], q_t[:, pair, :], k_t[:, pair, :, :],
                                                 start=True, stop=True)
                            last.then_inc(scores_done[half], 1)
                    if s.has(1):
                        b = s.item(1)
                        pe.wait_ge(ring_read, s.ring("p3", 1) + 1)
                        pe.wait_ge(v_ready, b + 1)
                        if s.has(1, 1):
                            pe.wait_ge(o_done, b)
                        if s.has(1, 3):
                            pe.wait_ge(logits_read, b - 2)
                        for h in range(H):
                            last = pe.matmul(psum_m[0][:, (DH + 1) * h:(DH + 1) * (h + 1)], p_t[:, h, :], v_one[:, h, :],
                                             start=True, stop=True)
                        last.then_inc(pv_done, 1)
                    if s.has(2):
                        b = s.item(2)
                        pe.wait_ge(ring_read, s.ring("o", 1) + 1)
                        if s.has(2, 1):
                            pe.wait_ge(x2_done, b)
                        if s.has(2, 3):
                            pe.wait_ge(rank_read, b - 2)
                        for c in range(KC):
                            last = pe.matmul(psum_m[1][:, 0:D], o_t[:, c, :], w_proj_sb[:, c, :], start=(c == 0), stop=(c == KC - 1))
                        last.then_inc(proj_done, 1)
                    if s.has(-1):
                        pe.wait_ge(q_lo, 2 * (s.item(-1) + 1))
                        parts = q_parts[:, :, :, :, :].rearrange("p (j h) c s d -> p j (h c s d)", h=2)
                        transposes(s, "q_a", [parts[:, j, :] for j in range(4)])
                        transposes(s, "q_b", [parts[:, j, :] for j in range(4, 8)])
                    if s.has(0):
                        pe.wait_ge(shifted_done[0], s.item(0) + 1)
                        for n in range(2):
                            transposes(s, f"p{n}", [shifted[0][:, 4 * n + j, :] for j in range(4)])
                    if s.has(1):
                        pe.wait_ge(o_done, s.item(1) + 1)
                        flat = o_sb[:, :, :].rearrange("p h d -> p (h d)")
                        transposes(s, "o", [flat[:, P * c:P * c + P] for c in range(KC)])
                    if s.has(3):
                        pe.wait_ge(norm2, s.item(3) + 1)
                        transposes(s, "n", [x2n[:, P * c:P * c + P] for c in range(KC)])
                    if s.has(4):
                        b = s.item(4)
                        pe.wait_ge(hot_done, b + 1)
                        if s.has(4, 1):
                            pe.wait_ge(taken_done, b)
                        pe.wait_ge(x2_done, min(b + 3, NB) if s.fixed else b + 3)
                        if s.has(4, 1):
                            pe.wait_ge(rank_read, b)
                        pe.matmul(psum_m[1][:, 384:384 + E], before[:, :], hot[s.side(4)][:, :], start=True, stop=False)
                        pe.matmul(psum_m[1][:, 384:384 + E], ones[:, :], taken[:, :], start=False, stop=True).then_inc(rank_done, 1)
                    if s.has(0):
                        pe.wait_ge(shifted_done[1], s.item(0) + 1)
                        for n in range(2, 4):
                            transposes(s, f"p{n}", [shifted[1][:, 4 * n - 8 + j, :] for j in range(4)])
                    if s.has(3):
                        b = s.item(3)
                        pe.wait_ge(ring_read, s.ring("n") + 1)
                        pe.wait_ge(o_done, min(b + 3, NB) if s.fixed else b + 3)
                        if s.has(3, 1):
                            pe.wait_ge(logits_read, b)
                        for c in range(KC):
                            last = pe.matmul(psum_m[0][:, 384:384 + E], x2n_t[:, c, :], wr_sb[:, c, :], start=(c == 0), stop=(c == KC - 1))
                        last.then_inc(logits_done, 1)
                walk(pe, FIRST_A, LAST_A, LOOP_A, NB, step)

            @block.vector
            def _(dve):
                dve.memset(k_t[:, :, :, :].bitcast(F32), 0.0).then_inc(consts_set, 1)
                dve.memset(taken[:, :], 0.0).then_inc(consts_set, 1)
                dve.memset(ones[:, :], 1.0).then_inc(consts_set, 1)
                dve.wait_ge(consts_in, 16 * 6)
                dve.tensor_copy(before[:, :], const("before")).then_inc(consts_set, 1)
                dve.wait_ge(consts_set, CONSTS_SET)

                def shift(s, half):
                    b = s.item(0)
                    dve.wait_ge(row_max, 2 * b + half + 1)
                    if s.has(0, 1):
                        dve.wait_ge(ring_full, s.ring(f"p{2 * half + 1}", 1) + 1)
                    dve.tensor_tensor(shifted[half][:, :, :], psum_s[half][:, :, :],
                                      repeat_last(smax[:, 8 * half:8 * half + 8], P), ALU.subtract).then_inc(shifted_done[half], 1)

                def largest(s, half):
                    b = s.item(0)
                    dve.wait_ge(scores_done[half], b + 1)
                    if s.has(0, 1):
                        dve.wait_ge(shifted_done[half], b)
                    dve.tensor_reduce(smax[:, 8 * half:8 * half + 8], psum_s[half][:, :, :], AX.X, ALU.max).then_inc(row_max, 1)

                def norm_chain(done, base, st, mv, ve, src):
                    def stats():
                        dve.bn_stats(st[:, :], src).then_inc(done, 1)

                    def moments():
                        dve.bn_aggr(mv[:, :], st[:, :]).then_inc(done, 1)

                    def variance():
                        dve.wait_ge(done, base + 2)
                        dve.tensor_scalar(ve[:, :], mv[:, 1:2], EPS, None, ALU.add).then_inc(done, 1)
                    return stats, moments, variance

                def step(s):
                    nw, nx, n0, n1, n2, n3, n4 = (s.has(lag) for lag in (-3, -2, 0, 1, 2, 3, 4))
                    b, p = s.item(-2), s.side(-2)
                    if nw:
                        bw, pw = s.item(-3), s.side(-3)
                        stats, moments, variance = norm_chain(stats1, CHAIN * bw, st1, mv1[pw], ve1[pw], x_sb[pw][:, :])
                        dve.wait_ge(x_in[pw], 16 * (s.turn(-3) + 1))
                        if s.has(-3, 1):
                            dve.wait_ge(stats1, CHAIN * bw)
                        if s.has(-3, 2):
                            dve.wait_ge(norm1, bw - 1)
                        stats()
                        dve.wait_ge(stats1, CHAIN * bw + 1)
                    if n0:
                        largest(s, 0)
                    if nw:
                        moments()
                    if n0:
                        shift(s, 0)
                    if nw:
                        if s.has(-3, 2):
                            dve.wait_ge(root1, bw - 1)
                        variance()
                    if n3:
                        p3 = s.side(3)
                        dve.wait_ge(root2, s.item(3) + 1)
                        if s.has(3, 1):
                            dve.wait_ge(ring_full, s.ring("n", 1) + 1)
                        dve.tensor_scalar(x2n[:, :], x2[p3][:, 0:D], mv2[p3][:, 0:1], rs2[p3][:, 0:1], ALU.subtract, ALU.mult).then_inc(norm2, 1)
                    if n1:
                        b1_ = s.item(1)
                        sums = psum_m[0][:, 0:H * (DH + 1)].rearrange("p (h e) -> p h e", h=H)
                        dve.wait_ge(pv_done, b1_ + 1)
                        if s.has(1, 1):
                            dve.wait_ge(o_done, b1_)
                        dve.reciprocal(recip[:, :], sums[:, :, DH]).then_inc(recip_done, 1)
                    if nx:
                        dve.wait_ge(root1, b + 1)
                        if s.has(-2, 1):
                            dve.wait_ge(q_lo, 2 * b)
                        dve.tensor_scalar(xn[:, :], x_sb[p][:, :], mv1[p][:, 0:1], rs1[p][:, 0:1], ALU.subtract, ALU.mult).then_inc(norm1, 1)
                    if n1:
                        dve.wait_ge(recip_done, b1_ + 1)
                        if s.has(1, 1):
                            dve.wait_ge(ring_full, s.ring("o", 1) + 1)
                        dve.tensor_tensor(o_sb[:, :, :], sums[:, :, 0:DH], repeat_last(recip[:, :], DH), ALU.mult).then_inc(o_done, 1)
                    if n0:
                        largest(s, 1)
                    if nx:
                        dve.wait_ge(norm1, b + 1)
                        if s.has(-2, 1):
                            dve.wait_ge(ring_full, s.ring("q_b") + 1)
                        dve.tensor_copy(q_parts[:, :, :, 0, :].bitcast(F32R),
                                        spread(xn[:, :].rearrange("p (h d) -> p h d", h=H), 2, 2)).then_inc(q_hi, 1)
                    if s.has(-1):
                        bk, pk = s.item(-1), s.side(-1)
                        dve.wait_ge(k_neg, bk + 1)
                        dve.wait_ge(k_in[pk], 32 * (s.turn(-1) + 1))
                        if s.has(-1, 1):
                            dve.wait_ge(scores_done[1], bk)
                        dve.tensor_tensor(k_t[64:P, :, 1, :], k_raw[pk][64:P, :, :], k_negated[64:P, :, :].bitcast(F32), ALU.add
                                          ).then_inc(k_ready[1], 1)
                    if n0:
                        shift(s, 1)
                    if n2:
                        b2_, p2 = s.item(2), s.side(2)
                        dve.wait_ge(proj_done, b2_ + 1)
                        dve.wait_ge(xb_done, b2_ + 1)
                        if s.has(2, 2):
                            dve.wait_ge(row_done, b2_ - 1)
                        dve.tensor_tensor(x2[p2][:, 0:D], psum_m[1][:, 0:D], xb[p2][:, :], ALU.add).then_inc(x2_done, 1)
                    if n3:
                        b3 = s.item(3)
                        dve.wait_ge(logits_done, b3 + 1)
                        if s.has(3, 1):
                            dve.wait_ge(choice, 3 * b3)
                        dve.tensor_tensor(logits[:, :], psum_m[0][:, 384:384 + E], b_r_sb[:, :], ALU.add).then_inc(logits_read, 1)
                    if n4:
                        b4, p4 = s.item(4), s.side(4)
                        dve.wait_ge(rank_done, b4 + 1)
                        if s.has(4, 1):
                            dve.wait_ge(place, b4)
                        dve.tensor_tensor(spot[:, :], psum_m[1][:, 384:384 + E], const("region"), ALU.add).then_inc(rank_read, 1)
                    if n3:
                        dve.wait_ge(logits_read, b3 + 1)
                    if n2:
                        stats_, moments_, variance_ = norm_chain(stats2, CHAIN * b2_, st2, mv2[p2], ve2[p2], x2[p2][:, 0:D])
                        dve.wait_ge(x2_done, b2_ + 1)
                        if s.has(2, 1):
                            dve.wait_ge(stats2, CHAIN * b2_)
                        if s.has(2, 2):
                            dve.wait_ge(norm2, b2_ - 1)
                        stats_()
                    if n3:
                        dve.max(top[:, :], logits[:, :]).then_inc(choice, 1)
                        dve.wait_ge(choice, 3 * b3 + 1)
                    if n2:
                        dve.wait_ge(stats2, CHAIN * b2_ + 1)
                    if n4:
                        dve.tensor_tensor(taken[:, :], taken[:, :], hot[p4][:, :], ALU.add).then_inc(taken_done, 1)
                    if n2:
                        moments_()
                    if n3:
                        dve.max_index(top_at[:, :], top[:, :], logits[:, :]).then_inc(choice, 1)
                    if n4:
                        dve.wait_ge(rank_read, b4 + 1)
                        if s.has(4, 1):
                            dve.wait_ge(place_done, b4)
                        dve.tensor_tensor_reduce(spot_x[:, :], spot[:, :], hot[p4][:, :], 1.0, 0.0, ALU.mult, ALU.add,
                                                 spot_f[:, :]).then_inc(place, 1)
                    if n2:
                        variance_()
                    if n3:
                        dve.wait_ge(choice, 3 * b3 + 2)
                        dve.tensor_copy(top_f[:, :], top_at[:, 0:1]).then_inc(choice, 1)
                    if n4:
                        dve.wait_ge(place, b4 + 1)
                        if s.has(4, 2):
                            dve.wait_ge(row_out[p4], 16 * s.turn(4))
                        dve.tensor_copy(spot_i[p4][:, :], spot_f[:, :]).then_inc(place_done, 1)
                    if n3:
                        dve.wait_ge(choice, 3 * b3 + 3)
                        dve.tensor_scalar(hot[s.side(3)][:, :], const("expert"), top_f[:, 0:1], None, ALU.is_equal).then_inc(hot_done, 1)
                walk(dve, FIRST_A, LAST_A, LOOP_A, NB, step)

        with ExitStack() as f:
            b2_sb = sb("b2_sb", [P, E, D], F32, f)
            w_now = [sb(f"w_now{i}", [P, 4, F], F32, f) for i in range(2)]
            b1_now = [sb(f"b1_now{i}", [P, FC], F32, f) for i in range(2)]
            t_in = [sb(f"t_in{i}", [P, ROW], F32, f) for i in range(2)]
            t_res = [sb(f"t_res{i}", [P, D + 1], F32, f) for i in range(2)]
            t_id = [sb(f"t_id{i}", [P, 1], U32, f) for i in range(2)]
            t_n = [sb(f"t_n{i}", [P, D], F32, f) for i in range(2)]
            t_nt = [sb(f"t_nt{i}", [P, KC, P], F32, f) for i in range(2)]
            hid = [sb(f"hid{i}", [P, FC, P], F32, f) for i in range(2)]
            t_out = [sb(f"t_out{i}", [P, D], F32, f) for i in range(2)]
            st = sb("st", [P, 6], F32, f)
            mv = sb("mv", [P, 2], F32, f)
            ve = sb("ve", [P, 1], F32, f)
            rs = sb("rs", [P, 1], F32, f)
            count = sb("count", [P, E], F32, f)
            pad_f = sb("pad_f", [P, E], F32, f)
            pad_i = [sb(f"pad_i{e}", [P, 1], U32, f) for e in range(E)]
            over = sb("over", [P, E, TOK // P], F32, f)
            tiles_of = sb("tiles_of", [P, E], F32, f)
            tiles_to = sb("tiles_to", [P, E], F32, f)
            tiles_at = sb("tiles_at", [P, E], F32, f)
            region_less = sb("region_less", [P, E], F32, f)
            past = sb("past", [P, TILES, E], F32, f)
            expert_f = sb("expert_f", [P, TILES], F32, f)
            is_expert = sb("is_expert", [P, TILES, E], F32, f)
            row_part = sb("row_part", [P, TILES, E], F32, f)
            row_f = sb("row_f", [P, TILES], F32, f)
            row_g = sb("row_g", [P, TILES], F32, f)
            row_h = sb("row_h", [P, TILES], F32, f)
            row_k = sb("row_k", [P, TILES], F32, f)
            tile_row = sb("tile_row", [P, TILES], I32, f)
            tile_expert = sb("tile_expert", [P, TILES], I32, f)

            counted, plan, pads_placed, pads_out, tables = (
                sem("counted"), sem("plan"), sem("pads_placed"), sem("pads_out"), sem("tables"))
            b2_in = sem("b2_in")
            t_loaded, t_done = sems("t_loaded"), sems("t_done")
            t_root = sem("t_root")
            t_ln, t_kept, t_turned, t_turned_read = sem("t_ln"), sem("t_kept"), sem("t_turned"), sem("t_turned_read")
            w1_set, w2_set = sem("w1_set"), sem("w2_set")
            hid_done, hid_read, y_done, y_read = sem("hid_done"), sem("hid_read"), sem("y_done"), sem("y_read")

            block = f.enter_context(nc.Block())

            @block.sync
            def _(sp):
                sp.dma_start(b2_sb[:, :, :].rearrange("p e d -> p (e d)"), spread(b2, 0, P)).then_inc(b2_in, 16)
                sp.wait_ge(pads_out, 16 * E)
                sp.wait_ge(tables, 2)

                def step(s):
                    if s.has(-2):
                        p = s.side(-2)
                        row = sp.value_load(tile_row[0:1, bass.ds(s.item(-2), 1)], min_val=0, max_val=SPARE)
                        if s.has(-2, 2):
                            sp.wait_ge(t_kept, 2 * (s.item(-2) - 1))
                        sp.dma_start(t_in[p][:, :], routed[bass.ds(row, P), :]).then_inc(t_loaded[p], 16)
                walk(sp, FIRST_F, LAST_F, LOOP_F, TILES, step)

            @block.gpsimd
            def _(pool):
                pool.wait_ge(pads_placed, E)
                for e in range(E):
                    pool.indirect_dma_start(
                        out=routed, out_offset=bass.IndirectOffsetOnAxis(ap=pad_i[e][:, 0:1], axis=0),
                        in_=pad[:, :], in_offset=None).then_inc(pads_out, 16)

                def step(s):
                    if s.has(2):
                        pool.wait_ge(y_read, 2 * (s.item(2) + 1))
                    if s.has(-1):
                        pool.wait_ge(t_ln, (CHAIN + 1) * s.item(-1) + CHAIN)
                        pool.tensor_tensor(rs[:, :], ve[:, :], const("power"), ALU.pow).then_inc(t_root, 1)
                    if s.has(2):
                        p = s.side(2)
                        pool.indirect_dma_start(
                            out=out_rows, out_offset=bass.IndirectOffsetOnAxis(ap=t_id[p][:, 0:1], axis=0),
                            in_=t_out[p][:, :], in_offset=None, bounds_check=TOK - 1, oob_is_err=False).then_inc(t_done[p], 16)
                walk(pool, FIRST_F, LAST_F, LOOP_F, TILES, step)
                for p in range(2):
                    pool.wait_ge(t_done[p], 16 * ((TILES + 1 - p) // 2))

            @block.scalar
            def _(act):
                act.wait_ge(tables, 2)
                act.wait_ge(experts_in, 16 * NB)

                def step(s):
                    if s.has(-1):
                        p = s.side(-1)
                        e = act.value_load(tile_expert[0:1, bass.ds(s.item(-1), 1)], min_val=0, max_val=E - 1)
                        if s.has(-1, 2):
                            act.wait_ge(y_done, s.item(-1) - 1)
                        act.activation(w_now[p][:, 2:4, :], w_sb[:, bass.ds(4 * e + 2, 2), :], ACT.Copy).then_inc(w2_set, 1)
                    if s.has(0):
                        p = s.side(0)
                        for c in range(FC):
                            if c % 4 == 0:
                                act.wait_ge(hid_done, 2 * s.item(0) + c // 4 + 1)
                                if s.has(0, 2) and c == 0:
                                    act.wait_ge(y_done, s.item(0) - 1)
                            bank = psum_s[p][:, :, :]
                            act.activation(hid[p][:, c, :], bank[:, c, :], ACT.Relu, bias=b1_now[p][:, c:c + 1]).then_inc(hid_read, 1)
                    if s.has(-1):
                        p = s.side(-1)
                        act.wait_ge(t_turned, s.item(-1) + 1)
                        if s.has(-1, 2):
                            act.wait_ge(hid_done, 2 * (s.item(-1) - 1))
                        act.activation(t_nt[p][:, :, :], psum_r[p][:, 0:D].rearrange("p (c t) -> p c t", c=KC), ACT.Copy).then_inc(t_turned_read, 1)
                walk(act, FIRST_F, LAST_F, LOOP_F, TILES, step)

            @block.tensor
            def _(pe):
                pe.matmul(psum_m[0][:, 0:E], ones[:, :], taken[:, :], start=True, stop=True).then_inc(counted, 1)

                def step(s):
                    if s.has(0):
                        b, p = s.item(0), s.side(0)
                        pe.wait_ge(t_turned_read, b + 1)
                        pe.wait_ge(w1_set, 2 * (b + 1))
                        if s.has(0, 2):
                            pe.wait_ge(hid_read, FC * (b - 1))
                        for c in range(FC):
                            for k in range(KC):
                                last = pe.matmul(psum_s[p][:, c, :], w_now[p][:, k, P * c:P * c + P], t_nt[p][:, k, :],
                                                 start=(k == 0), stop=(k == KC - 1))
                            if c % 4 == 3:
                                last.then_inc(hid_done, 1)
                    if s.has(1):
                        b, p = s.item(1), s.side(1)
                        pe.wait_ge(w2_set, b + 1)
                        pe.wait_ge(hid_read, FC * (b + 1))
                        if s.has(1, 2):
                            pe.wait_ge(y_read, 2 * (b - 1))
                        else:
                            pe.wait_ge(plan, 1)
                        w2 = w_now[p][:, 2:4, :].rearrange("p a (c d) -> p (a c) d", d=D)
                        for c in range(FC):
                            last = pe.matmul(psum_m[p][:, 0:D], hid[p][:, c, :], w2[:, c, :], start=(c == 0), stop=(c == FC - 1))
                        last.then_inc(y_done, 1)
                    if s.has(-1):
                        b, p = s.item(-1), s.side(-1)
                        pe.wait_ge(t_ln, (CHAIN + 1) * (b + 1))
                        if s.has(-1, 2):
                            pe.wait_ge(t_turned_read, b - 1)
                        for c in range(KC):
                            last = pe.transpose(psum_r[p][:, P * c:P * c + P], t_n[p][:, P * c:P * c + P], ident)
                        last.then_inc(t_turned, 1)
                walk(pe, FIRST_F, LAST_F, LOOP_F, TILES, step)

            @block.vector
            def _(dve):
                at = [0]

                def then(ins):
                    ins.then_inc(plan, 1)
                    at[0] += 1
                    dve.wait_ge(plan, at[0])

                dve.wait_ge(counted, 1)
                then(dve.tensor_copy(count[:, :], psum_m[0][:, 0:E]))
                then(dve.tensor_tensor(pad_f[:, :], count[:, :], const("pad_row"), ALU.add))
                for e in range(E):
                    dve.tensor_copy(pad_i[e][:, :], pad_f[:, e:e + 1]).then_inc(pads_placed, 1)
                then(dve.tensor_tensor(over[:, :, :], repeat_last(count[:, :], TOK // P), spread(const("full_rows"), 1, E), ALU.is_gt))
                then(dve.tensor_reduce(tiles_of[:, :], over[:, :, :], AX.X, ALU.add))
                then(dve.tensor_tensor_scan(tiles_to[:, :], tiles_of[:, :], tiles_of[:, :], 0.0, ALU.add, ALU.bypass))
                then(dve.tensor_tensor(tiles_at[:, :], tiles_to[:, :], tiles_of[:, :], ALU.subtract))
                then(dve.scalar_tensor_tensor(out=region_less[:, :], in0=tiles_at[:, :], scalar=-float(P), in1=const("region"),
                                              op0=ALU.mult, op1=ALU.add))
                then(dve.tensor_tensor(past[:, :, :], spread(tiles_to[:, :], 1, TILES), repeat_last(const("tile"), E), ALU.is_le))
                then(dve.tensor_reduce(expert_f[:, :], past[:, :, :], AX.X, ALU.add))
                then(dve.tensor_tensor(is_expert[:, :, :], repeat_last(expert_f[:, :], E), spread(const("expert"), 1, TILES), ALU.is_equal))
                then(dve.tensor_tensor(row_part[:, :, :], is_expert[:, :, :], spread(region_less[:, :], 1, TILES), ALU.mult))
                then(dve.tensor_reduce(row_f[:, :], row_part[:, :, :], AX.X, ALU.add))
                then(dve.tensor_tensor(row_g[:, :], row_f[:, :], const("tile_row"), ALU.add))
                then(dve.tensor_scalar(row_h[:, :], expert_f[:, :], float(E), float(SPARE), ALU.is_ge, ALU.mult))
                then(dve.tensor_tensor(row_k[:, :], row_g[:, :], row_h[:, :], ALU.add))
                dve.tensor_scalar(tile_row[:, :], row_k[:, :], float(SPARE), None, ALU.min).then_inc(tables, 1)
                dve.tensor_scalar(tile_expert[:, :], expert_f[:, :], float(E - 1), None, ALU.min).then_inc(tables, 1)
                dve.wait_ge(tables, 2)
                dve.wait_ge(experts_in, 16 * NB)
                dve.wait_ge(b2_in, 16)

                def step(s):
                    if s.has(-1):
                        b, p = s.item(-1), s.side(-1)
                        e = dve.value_load(tile_expert[0:1, bass.ds(b, 1)], min_val=0, max_val=E - 1)
                        base = (CHAIN + 1) * b
                        dve.wait_ge(t_loaded[p], 16 * (s.turn(-1) + 1))
                        if s.has(-1, 1):
                            dve.wait_ge(t_ln, base)
                        dve.bn_stats(st[:, :], t_in[p][:, 0:D]).then_inc(t_ln, 1)
                        if s.has(-1, 2):
                            dve.wait_ge(hid_done, 2 * (b - 1))
                            dve.wait_ge(hid_read, FC * (b - 1))
                        dve.wait_ge(t_ln, base + 1)
                        dve.tensor_copy(b1_now[p][:, :], b1_sb[:, bass.ds(e, 1), :].rearrange("p a c -> p (a c)")).then_inc(w1_set, 1)
                        dve.bn_aggr(mv[:, :], st[:, :]).then_inc(t_ln, 1)
                        dve.wait_ge(t_ln, base + 2)
                        dve.tensor_scalar(ve[:, :], mv[:, 1:2], EPS, None, ALU.add).then_inc(t_ln, 1)
                        dve.tensor_copy(w_now[p][:, 0:2, :], w_sb[:, bass.ds(4 * e, 2), :]).then_inc(w1_set, 1)
                        dve.wait_ge(t_root, b + 1)
                        if s.has(-1, 2):
                            dve.wait_ge(t_turned, b - 1)
                        dve.tensor_scalar(t_n[p][:, :], t_in[p][:, 0:D], mv[:, 0:1], rs[:, 0:1], ALU.subtract, ALU.mult).then_inc(t_ln, 1)
                    if s.has(1):
                        q = s.side(1)
                        dve.wait_ge(y_done, s.item(1) + 1)
                        if s.has(1, 2):
                            dve.wait_ge(t_done[q], 16 * s.turn(1))
                        dve.wait_ge(t_kept, 2 * (s.item(1) + 1))
                        dve.tensor_tensor(t_out[q][:, :], psum_m[q][:, 0:D], t_res[q][:, 0:D], ALU.add).then_inc(y_read, 1)
                        dve.tensor_copy(t_id[q][:, :], t_res[q][:, D:D + 1]).then_inc(y_read, 1)
                    if s.has(-1):
                        if s.has(-1, 2):
                            dve.wait_ge(y_read, 2 * (b - 1))
                        dve.tensor_tensor(t_res[p][:, 0:D], t_in[p][:, 0:D], b2_sb[:, bass.ds(e, 1), :].rearrange("p a d -> p (a d)"),
                                          ALU.add).then_inc(t_kept, 1)
                        dve.tensor_copy(t_res[p][:, D:D + 1], t_in[p][:, D:D + 1]).then_inc(t_kept, 1)
                walk(dve, FIRST_F, LAST_F, LOOP_F, TILES, step)


def constants():
    import numpy as np
    t = np.zeros((P, CONST_WIDTH), np.float32)

    def put(name, value):
        a, b = CONST_COLS[name]
        t[:, a:b] = value
    lane = np.arange(P)
    put("ident", np.eye(P))
    put("before", lane[:, None] < lane[None, :])
    put("region", REGION * np.arange(E)[None])
    put("pad_row", REGION * np.arange(E)[None] + lane[:, None])
    put("expert", np.arange(E)[None])
    put("full_rows", P * np.arange(TOK // P)[None])
    put("tile", np.arange(TILES)[None])
    put("tile_row", P * np.arange(TILES)[None])
    put("minus_hi", -(lane // 32 % 2)[:, None])
    put("lane", lane[:, None])
    put("power", -0.5)
    put("round", 2 * P)
    return t


def kernel(x, ctx_1024, L0_xattn_w_proj, L0_xattn_b_proj, L0_ffn_Wr, L0_ffn_br, L0_ffn_W1, L0_ffn_b1, L0_ffn_W2, L0_ffn_b2):
    import numpy as np
    import concourse.bacc as bacc
    from concourse.bass_utils import run_bass_kernel_spmd

    x = np.asarray(x)
    ctx = np.asarray(ctx_1024)
    heads = ctx.reshape(NB, P, PAIRS, 2, DH).transpose(0, 3, 4, 2, 1)
    w1 = np.asarray(L0_ffn_W1).transpose(0, 2, 1).reshape(E, 2, P, F)
    w2 = np.asarray(L0_ffn_W2).transpose(0, 2, 1).reshape(E, 2, FC // 2, P, D).transpose(0, 1, 3, 2, 4).reshape(E, 2, P, F)
    arrays = {
        "x": x,
        "ctx_rows": ctx.reshape(TOK, D),
        "ctx_heads": heads,
        "w_proj_t": np.asarray(L0_xattn_w_proj).T,
        "b_proj": np.asarray(L0_xattn_b_proj).reshape(1, D),
        "wr_t": np.asarray(L0_ffn_Wr).T,
        "b_r": np.asarray(L0_ffn_br).reshape(1, E),
        "experts": np.concatenate([w1, w2], axis=1).reshape(4 * E, P, F),
        "b1_cols": np.asarray(L0_ffn_b1).reshape(E, FC, P).transpose(2, 0, 1),
        "b2": np.asarray(L0_ffn_b2).reshape(1, E * D),
        "consts": constants(),
    }
    arrays = {f"in_{k}": np.ascontiguousarray(v) for k, v in arrays.items()}
    nc = bacc.Bacc("TRN2", target_bir_lowering=False, num_devices=1)
    args = [nc.dram_tensor(k, v.shape, mybir.dt.from_np(v.dtype), kind="ExternalInput").ap() for k, v in arrays.items()]
    out = nc.dram_tensor("out", (NB, P, D), F32, kind="ExternalOutput").ap()
    build(nc, *args, out)
    r = run_bass_kernel_spmd(nc, [arrays], core_ids=[0])
    return r.results[0]["out"]
```

```python
from contextlib import ExitStack

import concourse.bass as bass
from concourse import mybir

P = 128
D = 256
H = 16
DH = D // H
PAIRS = H // 2
NB = 32
TOK = NB * P
E = 8
F = 1024
KC = D // P
FC = F // P
TILES = TOK // P + E - 1
REGION = TOK + P
SPARE = E * REGION
ROW = D + 16
NOWHERE = 1.0e6
SCALE = 1.0 / DH ** 0.5
EPS = 1e-5

F32 = mybir.dt.float32
F32R = mybir.dt.float32r
BF16 = mybir.dt.bfloat16
I32 = mybir.dt.int32
U32 = mybir.dt.uint32
ALU = mybir.AluOpType
ACT = mybir.ActivationFunctionType
AX = mybir.AxisListType

CONST_COLS = {}
CONST_WIDTH = 0
for _name, _n in (("ident", P), ("before", P), ("region", E), ("taken_first", E), ("count_back", E), ("pad_row", E), ("expert", E),
                  ("full_rows", TOK // P), ("tile", TILES), ("tile_row", TILES), ("minus_hi", 1), ("lane", 1), ("power", 1), ("round", 1),
                  ("part0", 1), ("part1", 1), ("part2", 1)):
    CONST_COLS[_name] = (CONST_WIDTH, CONST_WIDTH + _n)
    CONST_WIDTH += _n

RING = (("p2", 1), ("p3", 1), ("p0", 0), ("p1", 0), ("q_a", -1), ("q_b", -1), ("n", 3), ("o", 1))
UNROLL = 4
FIRST_A, LAST_A = -5, NB + 4
LOOP_A = (2, 7)
FIRST_F, LAST_F = -3, TILES + 1
LOOP_F = (1, 9)


def uses_before(step):
    return sum(1 for s in range(FIRST_A, step) for _, lag in RING if 0 <= s - lag < NB)


STEADY = uses_before(UNROLL * LOOP_A[0]) - len(RING) * UNROLL * LOOP_A[0]


class Step:

    def __init__(self, round_, place, count):
        self.round, self.place, self.count = round_, place, count
        self.fixed = isinstance(round_, int)
        self.number = UNROLL * round_ + place

    def has(self, lag, least=0):
        return not self.fixed or least <= self.number - lag < self.count

    def item(self, lag):
        return self.number - lag

    def side(self, lag, n=2):
        return (self.place - lag) % n

    def turn(self, lag, n=2):
        return UNROLL // n * self.round + (self.place - lag) // n

    def ring(self, name, back=0):
        at = [n for n, _ in RING].index(name)
        if not self.fixed:
            return self.number * len(RING) + (STEADY - back * len(RING) + at)
        s = self.number - back
        return uses_before(s) + sum(1 for _, lag in RING[:at] if 0 <= s - lag < NB)

    def bank(self, name):
        if self.fixed:
            return self.ring(name) % 2
        return (STEADY + [n for n, _ in RING].index(name)) % 2


def walk(engine, first, last, loop, count, body):
    for s in range(first, UNROLL * loop[0]):
        body(Step(s // UNROLL, s % UNROLL, count))
    with engine.Fori(loop[0], loop[1]) as round_:
        for place in range(UNROLL):
            body(Step(round_, place, count))
    for s in range(UNROLL * loop[1], last + 1):
        body(Step(s // UNROLL, s % UNROLL, count))


def spread(ap, axis, n):
    names = [f"a{i}" for i in range(len(ap.shape))]
    inner = names[:axis] + [f"(o {names[axis]})"] + names[axis + 1:]
    out = names[:axis] + ["o", names[axis]] + names[axis + 1:]
    v = ap.rearrange(" ".join(inner) + " -> " + " ".join(out), o=1)
    shape = list(v.shape)
    shape[axis] = n
    return v.to_broadcast(shape)


def repeat_last(ap, n):
    names = [f"a{i}" for i in range(len(ap.shape))]
    v = ap.rearrange(" ".join(names[:-1] + [f"({names[-1]} o)"]) + " -> " + " ".join(names + ["o"]), o=1)
    return v.to_broadcast(list(ap.shape) + [n])


def build(nc, x, ctx_rows, ctx_heads, w_proj_t, b_proj, wr_t, b_r, experts, b1_cols, b2, consts, out):
    routed = nc.dram_tensor("routed", (SPARE + P, ROW), F32).ap()
    x_rows = x.rearrange("b t d -> (b t) d")
    out_rows = out.rearrange("b t d -> (b t) d")

    with ExitStack() as ctx:
        def sb(name, shape, dt, where=None):
            return (where or ctx).enter_context(nc.sbuf_tensor(name, shape, dt))

        def sem(name):
            return ctx.enter_context(nc.semaphore(name))

        def sems(name):
            return [sem(f"{name}{i}") for i in range(2)]

        psum_s = [ctx.enter_context(nc.psum_tensor(f"scores{h}", [P, PAIRS, P], F32)) for h in range(2)]
        psum_r = [ctx.enter_context(nc.psum_tensor(f"transfer{i}", [P, 512], F32)) for i in range(2)]
        psum_m = [ctx.enter_context(nc.psum_tensor(f"sums{i}", [P, 512], F32)) for i in range(2)]

        cst = sb("cst", [P, CONST_WIDTH], F32)

        def const(name):
            a, b = CONST_COLS[name]
            return cst[:, a:b]

        ident = const("ident")
        before = sb("before", [P, P], BF16)
        ones_bf = sb("ones_bf", [P, P], BF16)
        b_proj_parts = sb("b_proj_parts", [P, D], BF16)
        w_proj_sb = sb("w_proj_sb", [P, KC, D], F32)
        wr_sb = sb("wr_sb", [P, KC, E], F32)
        b1_sb = sb("b1_sb", [P, E, FC], F32)
        w_sb = sb("w_sb", [P, 4 * E, F], F32)
        taken = sb("taken", [P, E], BF16)
        pad = sb("pad", [P, ROW], F32)

        consts_in = sem("consts_in")
        consts_set = sem("consts_set")
        experts_in = sem("experts_in")
        spare_written = sem("spare_written")
        x_in, row_out = ([sem(f"{n}{i}") for i in range(4)] for n in ("x_in", "row_out"))
        k_in, v_in, xr_in = sems("k_in"), sems("v_in"), sems("xr_in")
        stats1, root1, shift1, norm1 = sem("stats1"), sem("root1"), sem("shift1"), sem("norm1")
        q_lo = sem("q_lo")
        k_neg, k_split, k_ready = sem("k_neg"), sem("k_split"), sem("k_ready")
        scores_done = sems("scores_done")
        row_max = sem("row_max")
        shifted_done = sems("shifted_done")
        ring_full, ring_read = sem("ring_full"), sem("ring_read")
        pv_done, pv_read, back_done = sem("pv_done"), sem("pv_read"), sem("back_done")
        recip_done, o_done = sem("recip_done"), sem("o_done")
        proj_done, x2_done = sem("proj_done"), sem("x2_done")
        stats2, root2, shift2, norm2 = sem("stats2"), sem("root2"), sem("shift2"), sem("norm2")
        logits_done, logits_read = sem("logits_done"), sem("logits_read")
        choice, hot_done = sem("choice"), sem("hot_done")
        rank_done, taken_done, place, place_done = sem("rank_done"), sem("taken_done"), sem("place"), sem("place_done")
        number_set = sem("number_set")

        CHAIN = 3
        CONSTS_IN = 16 * 6
        CONSTS_SET = 7
        NUMBERS = 9
        SMALL = 384
        QUAD = 4

        a = ExitStack()
        with a:
            b_proj_sb = sb("b_proj_sb", [P, D], F32, a)
            b_r_sb = sb("b_r_sb", [P, E], F32, a)
            x_sb = [sb(f"x_sb{i}", [P, D], F32, a) for i in range(4)]
            xn = sb("xn", [P, D], F32, a)
            q_parts = [sb(f"q_parts{i}", [P, H, 2, 2, DH], F32, a) for i in range(2)]
            q_t = sb("q_t", [P, PAIRS, P], F32R, a)
            k_raw = [sb(f"k_raw{i}", [P, PAIRS, P], F32, a) for i in range(2)]
            k_parts = [sb(f"k_parts{i}", [P, PAIRS, P], F32R, a) for i in range(2)]
            k_t = sb("k_t", [P, PAIRS, 2, P], F32R, a)
            shifted = [sb(f"shifted{i}", [P, PAIRS, P], F32, a) for i in range(2)]
            p_t = sb("p_t", [P, H, P], F32, a)
            v_one = [sb(f"v_one{i}", [P, H, DH + 1], F32, a) for i in range(2)]
            xr_sb = [sb(f"xr_sb{i}", [P, D], F32, a) for i in range(2)]
            pv_t = sb("pv_t", [P, H // QUAD, P], F32, a)
            o_sb = sb("o_sb", [P, H, DH], F32, a)
            o_t = sb("o_t", [P, KC, P], F32, a)
            row = [sb(f"row{i}", [P, ROW], F32, a) for i in range(4)]
            x2n = sb("x2n", [P, D], F32, a)
            x2n_t = sb("x2n_t", [P, KC, P], F32, a)
            st1, st2 = sb("st1", [P, 6], F32, a), sb("st2", [P, 6], F32, a)
            mv1, mv2 = ([sb(f"mv{n}{i}", [P, 2], F32, a) for i in range(2)] for n in (1, 2))
            ve1, ve2 = ([sb(f"ve{n}{i}", [P, 1], F32, a) for i in range(2)] for n in (1, 2))
            rs1, rs2 = ([sb(f"rs{n}{i}", [P, 1], F32, a) for i in range(2)] for n in (1, 2))
            nm1, nm2 = ([sb(f"nm{n}{i}", [P, 1], F32, a) for i in range(2)] for n in (1, 2))
            smax = sb("smax", [P, H], F32, a)
            recip = sb("recip", [P, H], F32, a)
            logits = sb("logits", [P, E], F32, a)
            top = sb("top", [P, E], F32, a)
            top_at = sb("top_at", [P, E], U32, a)
            top_f = sb("top_f", [P, 1], F32, a)
            hot = [sb(f"hot{i}", [P, E], BF16, a) for i in range(2)]
            spot_x = sb("spot_x", [P, E], F32, a)
            spot_f = sb("spot_f", [P, 1], F32, a)
            spot_i = [sb(f"spot_i{i}", [P, 1], U32, a) for i in range(4)]

            block = a.enter_context(nc.Block())

            @block.sync
            def _(sp):
                sp.dma_start(cst[:, :], consts).then_inc(consts_in, 16)

                def step(s):
                    if s.has(-1, 1):
                        sp.wait_ge(scores_done[1], s.item(-1))
                    elif s.has(-1):
                        sp.wait_ge(consts_set, CONSTS_SET)
                    elif s.has(0):
                        sp.wait_ge(pv_done, s.item(0) - 1)
                    if s.has(0):
                        p = s.side(0)
                        sp.dma_start(v_one[p][:, :, :].rearrange("p h e -> p (h e)"), ctx_rows[bass.ds(s.item(0) * P, P), :]).then_inc(v_in[p], 16)
                    if s.has(-1):
                        p = s.side(-1)
                        sp.wait_ge(k_split, s.item(-1) + 1)
                        for h in range(2):
                            sp.dma_start(k_t[64 * h:64 * h + 64, :, h, :].bitcast(F32), k_parts[p][64 * h:64 * h + 64, :, :].bitcast(F32)).then_inc(k_ready, 16)
                    if s.has(-5):
                        p = s.side(-5, 4)
                        if s.has(-5, 4):
                            sp.wait_ge(norm1, s.item(-5) - 3)
                        sp.dma_start(x_sb[p][:, :], x_rows[bass.ds(s.item(-5) * P, P), :]).then_inc(x_in[p], 16)
                    if s.has(1):
                        p = s.side(1)
                        if s.has(1, 2):
                            sp.wait_ge(x2_done, s.item(1) - 1)
                        sp.dma_start(xr_sb[p][:, :], x_rows[bass.ds(s.item(1) * P, P), :]).then_inc(xr_in[p], 16)
                    if s.has(-4):
                        p = s.side(-4)
                        if s.has(-4, 2):
                            sp.wait_ge(k_split, s.item(-4) - 1)
                        for h in range(2):
                            sp.dma_start(k_raw[p][64 * h:64 * h + 64, :, :],
                                         spread(ctx_heads[bass.ds(s.item(-4), 1), h].rearrange("b d j s -> (b d) (j s)"), 0, 4)
                                         ).then_inc(k_in[p], 16)
                    if s.has(0):
                        sp.dma_start(w_sb[:, bass.ds(s.item(0), 1), :].rearrange("p c f -> p (c f)"),
                                     experts[bass.ds(s.item(0), 1)].rearrange("c p f -> (c p) f")).then_inc(experts_in, 16)
                walk(sp, FIRST_A, LAST_A, (LOOP_A[0], LOOP_A[1] - 1), NB, step)

            @block.gpsimd
            def _(pool):
                pool.memset(pad[:, :], 0.0).then_inc(number_set, 1)
                for p in range(4):
                    pool.memset(row[p][:, D:ROW], 0.0).then_inc(number_set, 1)
                pool.wait_ge(consts_in, CONSTS_IN)
                pool.wait_ge(number_set, 5)
                pool.memset(pad[:, D:D + 1], NOWHERE).then_inc(consts_set, 1)
                for p in range(4):
                    pool.tensor_scalar(row[p][:, D:D + 1], const("lane"), float((p - UNROLL) * P), None, ALU.add).then_inc(number_set, 1)

                def step(s):
                    if s.has(3):
                        p = s.side(3)
                        pool.wait_ge(stats2, CHAIN * (s.item(3) + 1))
                        if s.has(3, 2):
                            pool.wait_ge(norm2, s.item(3) - 1)
                        pool.tensor_tensor(rs2[p][:, :], ve2[p][:, :], const("power"), ALU.pow).then_inc(root2, 1)
                    if s.has(-3):
                        q = s.side(-3)
                        pool.wait_ge(stats1, CHAIN * (s.item(-3) + 1))
                        if s.has(-3, 2):
                            pool.wait_ge(norm1, s.item(-3) - 1)
                        pool.tensor_tensor(rs1[q][:, :], ve1[q][:, :], const("power"), ALU.pow).then_inc(root1, 1)
                    if s.has(3):
                        pool.wait_ge(root2, s.item(3) + 1)
                    if s.has(-3):
                        pool.wait_ge(root1, s.item(-3) + 1)
                    if s.has(3):
                        r = s.side(3, 4)
                        if s.has(3, 4):
                            pool.wait_ge(row_out[r], 16 * s.turn(3, 4))
                        else:
                            pool.wait_ge(number_set, 6 + r)
                        pool.tensor_tensor(row[r][:, D:D + 1], row[r][:, D:D + 1], const("round"), ALU.add).then_inc(number_set, 1)
                        pool.tensor_scalar(nm2[p][:, :], mv2[p][:, 0:1], rs2[p][:, 0:1], -1.0, ALU.mult, ALU.mult).then_inc(shift2, 1)
                    if s.has(-3):
                        pool.tensor_scalar(nm1[q][:, :], mv1[q][:, 0:1], rs1[q][:, 0:1], -1.0, ALU.mult, ALU.mult).then_inc(shift1, 1)
                    if s.has(-2):
                        p = s.side(-2)
                        pool.wait_ge(k_neg, s.item(-2) + 1)
                        pool.tensor_tensor(k_parts[p][:, :, :], k_raw[p][:, :, :], k_parts[p][:, :, :].bitcast(F32), ALU.add
                                           ).then_inc(k_split, 1)
                        pool.wait_ge(norm1, s.item(-2) + 1)
                        lo = [q_parts[p][:, :, c, 1, :] for c in range(2)]
                        hi = [q_parts[p][:, :, c, 0, :] for c in range(2)]
                        x_heads = xn[:, :].rearrange("p (h d) -> p h d", h=H)
                        pool.tensor_tensor(lo[0], x_heads, hi[0], ALU.subtract).then_inc(q_lo, 1)
                    if s.has(5):
                        pool.wait_ge(number_set, NUMBERS + s.item(5) + 1)
                        pool.wait_ge(place_done, s.item(5) + 1)
                    if s.has(-2):
                        pool.tensor_tensor(lo[1], x_heads, hi[1], ALU.subtract).then_inc(q_lo, 1)
                    if s.has(5):
                        r = s.side(5, 4)
                        pool.indirect_dma_start(
                            out=routed, out_offset=bass.IndirectOffsetOnAxis(ap=spot_i[r][:, 0:1], axis=0),
                            in_=row[r][:, :], in_offset=None).then_inc(row_out[r], 16)
                walk(pool, FIRST_A, LAST_A, LOOP_A, NB, step)
                for p in range(4):
                    pool.wait_ge(row_out[p], 16 * (NB // 4))
                pool.wait_ge(spare_written, 16)

            @block.scalar
            def _(act):
                act.dma_start(b_proj_sb[:, :], spread(b_proj, 0, P)).then_inc(consts_in, 16)
                act.dma_start(w_proj_sb[:, :, :], w_proj_t.rearrange("(c p) n -> p c n", p=P)).then_inc(consts_in, 16)
                act.dma_start(wr_sb[:, :, :], wr_t.rearrange("(c p) n -> p c n", p=P)).then_inc(consts_in, 16)
                act.dma_start(b_r_sb[:, :], spread(b_r, 0, P)).then_inc(consts_in, 16)
                act.dma_start(b1_sb[:, :, :], b1_cols).then_inc(consts_in, 16)
                act.wait_ge(consts_set, CONSTS_SET)
                act.dma_start(routed[SPARE:SPARE + P, :], pad[:, :]).then_inc(spare_written, 16)

                def read_ring(s, name, out, func, scale=1.0):
                    n = s.ring(name)
                    act.wait_ge(ring_full, n + 1)
                    src = psum_r[s.bank(name)][:, 0:out.free_size()]
                    if len(out.shape) == 3:
                        src = src.rearrange("p (c t) -> p c t", c=out.shape[1])
                    act.activation(out, src, func, scale=scale).then_inc(ring_read, 1)

                def step(s):
                    if s.has(1):
                        if s.has(1, 1):
                            act.wait_ge(pv_done, s.item(1))
                        for n in range(2, 4):
                            read_ring(s, f"p{n}", p_t[:, 4 * n:4 * n + 4, :], ACT.Exp, scale=SCALE)
                    if s.has(3):
                        p, r = s.side(3), s.side(3, 4)
                        act.wait_ge(shift2, s.item(3) + 1)
                        if s.has(3, 1):
                            act.wait_ge(ring_full, s.ring("n", 1) + 1)
                        act.activation(x2n[:, :], row[r][:, 0:D], ACT.Identity, bias=nm2[p][:, 0:1], scale=rs2[p][:, 0:1]).then_inc(norm2, 1)
                    if s.has(-2):
                        p, r = s.side(-2), s.side(-2, 4)
                        act.wait_ge(shift1, s.item(-2) + 1)
                        if s.has(-2, 2):
                            act.wait_ge(ring_full, s.ring("q_b", 1) + 1)
                        act.activation(q_parts[p][:, :, :, 0, :].bitcast(F32R),
                                       spread(x_sb[r][:, :].rearrange("p (h d) -> p h d", h=H), 2, 2),
                                       ACT.Identity, bias=nm1[p][:, 0:1], scale=rs1[p][:, 0:1])
                        if s.has(-2, 1):
                            act.wait_ge(q_lo, 2 * s.item(-2))
                        act.activation(xn[:, :], x_sb[r][:, :], ACT.Identity, bias=nm1[p][:, 0:1], scale=rs1[p][:, 0:1]).then_inc(norm1, 1)
                    if s.has(1):
                        act.wait_ge(pv_done, s.item(1) + 1)
                        if s.has(1, 1):
                            act.wait_ge(back_done, s.item(1))
                        act.activation(pv_t[:, :, :], psum_m[0][:, :].rearrange("p (g t) -> p g t", t=P), ACT.Copy).then_inc(pv_read, 1)
                    if s.has(0):
                        for n in range(2):
                            read_ring(s, f"p{n}", p_t[:, 4 * n:4 * n + 4, :], ACT.Exp, scale=SCALE)
                    if s.has(-1):
                        if s.has(-1, 1):
                            act.wait_ge(scores_done[1], s.item(-1))
                        for n, name in enumerate(("q_a", "q_b")):
                            read_ring(s, name, q_t[:, 4 * n:4 * n + 4, :], ACT.Copy)
                    if s.has(3):
                        if s.has(3, 1):
                            act.wait_ge(logits_done, s.item(3))
                        read_ring(s, "n", x2n_t[:, :, :], ACT.Copy)
                    if s.has(1):
                        if s.has(1, 1):
                            act.wait_ge(proj_done, s.item(1))
                        read_ring(s, "o", o_t[:, :, :], ACT.Copy)
                    if s.has(-3):
                        p = s.side(-3)
                        act.wait_ge(k_in[p], 32 * (s.turn(-3) + 1))
                        if s.has(-3, 2):
                            act.wait_ge(k_ready, 32 * (s.item(-3) - 1))
                        act.activation(k_parts[p][:, :, :], k_raw[p][:, :, :], ACT.Copy, scale=const("minus_hi")).then_inc(k_neg, 1)
                walk(act, FIRST_A, LAST_A, LOOP_A, NB, step)

            @block.tensor
            def _(pe):
                pe.wait_ge(consts_in, CONSTS_IN)
                pe.wait_ge(consts_set, CONSTS_SET)

                def transposes(s, name, parts):
                    n = s.ring(name)
                    if not s.fixed or n >= 2:
                        pe.wait_ge(ring_read, n - 1)
                    for c, part in enumerate(parts):
                        last = pe.transpose(psum_r[s.bank(name)][:, P * c:P * c + P], part, ident)
                    last.then_inc(ring_full, 1)

                def scores(s, half):
                    if s.has(-1, 1):
                        pe.wait_ge(shifted_done[half], s.item(-1))
                    for j in range(PAIRS // 2):
                        pair = PAIRS // 2 * half + j
                        last = pe.matmul(psum_s[half][:, 2 * j:2 * j + 2, :], q_t[:, pair, :], k_t[:, pair, :, :],
                                         start=True, stop=True)
                    last.then_inc(scores_done[half], 1)

                def step(s):
                    small = psum_m[1][:, SMALL:SMALL + 2 * E]
                    if s.has(1):
                        pe.wait_ge(shifted_done[1], s.item(1) + 1)
                        for n in range(2, 4):
                            transposes(s, f"p{n}", [shifted[1][:, 4 * n - 8 + j, :] for j in range(4)])
                    if s.has(2):
                        pe.wait_ge(o_done, s.item(2) + 1)
                    if s.has(5):
                        b = s.item(5)
                        pe.wait_ge(hot_done, b + 1)
                        if s.has(5, 1):
                            pe.wait_ge(taken_done, b)
                            pe.wait_ge(place, b)
                        pe.matmul(small[:, 0:E], before[:, :], hot[s.side(5)][:, :], start=True, stop=False)
                        pe.matmul(small[:, 0:E], ones_bf[:, :], taken[:, :], start=False, stop=True).then_inc(rank_done, 1)
                    if s.has(4):
                        pe.wait_ge(ring_read, s.ring("n", 1) + 1)
                        if s.has(4, 1):
                            pe.wait_ge(logits_read, s.item(4))
                        for c in range(KC):
                            last = pe.matmul(small[:, E:2 * E], x2n_t[:, c, :], wr_sb[:, c, :], start=(c == 0), stop=(c == KC - 1))
                        last.then_inc(logits_done, 1)
                    if s.has(2):
                        pe.wait_ge(ring_read, s.ring("o", 1) + 1)
                        pe.matmul(psum_m[1][:, 0:D], ones_bf[:, :], b_proj_parts[:, :], start=True, stop=False)
                        for c in range(KC):
                            last = pe.matmul(psum_m[1][:, 0:D], o_t[:, c, :], w_proj_sb[:, c, :], start=False, stop=(c == KC - 1))
                        last.then_inc(proj_done, 1)
                    if s.has(1):
                        b = s.item(1)
                        pe.wait_ge(ring_read, s.ring("p3") + 1)
                        pe.wait_ge(v_in[s.side(1)], 16 * (s.turn(1) + 1))
                        if s.has(1, 1):
                            pe.wait_ge(pv_read, b)
                        for h in range(H):
                            j, g = h % QUAD, h // QUAD
                            last = pe.matmul(psum_m[0][32 * j:32 * j + DH + 1, P * g:P * g + P], v_one[s.side(1)][:, h, :], p_t[:, h, :],
                                             start=True, stop=True)
                        last.then_inc(pv_done, 1)
                    if s.has(0):
                        pe.wait_ge(shifted_done[0], s.item(0) + 1)
                        for n in range(2):
                            transposes(s, f"p{n}", [shifted[0][:, 4 * n + j, :] for j in range(4)])
                    if s.has(1):
                        pe.wait_ge(pv_read, s.item(1) + 1)
                        if s.has(2):
                            pe.wait_ge(x2_done, s.item(2) + 1)
                        if s.has(4):
                            pe.wait_ge(logits_read, s.item(4) + 1)
                        if s.has(5):
                            pe.wait_ge(place, s.item(5) + 1)
                        for g in range(H // QUAD):
                            last = pe.transpose(psum_m[1][:, P * g:P * g + P], pv_t[:, g, :], ident)
                        last.then_inc(back_done, 1)
                    if s.has(-1):
                        pe.wait_ge(q_lo, 2 * (s.item(-1) + 1))
                        parts = q_parts[s.side(-1)][:, :, :, :, :].rearrange("p (j h) c s d -> p j (h c s d)", h=2)
                        transposes(s, "q_a", [parts[:, j, :] for j in range(4)])
                        transposes(s, "q_b", [parts[:, j, :] for j in range(4, 8)])
                    if s.has(3):
                        pe.wait_ge(norm2, s.item(3) + 1)
                        transposes(s, "n", [x2n[:, P * c:P * c + P] for c in range(KC)])
                    if s.has(-1):
                        pe.wait_ge(ring_read, s.ring("q_b") + 1)
                        pe.wait_ge(k_ready, 32 * (s.item(-1) + 1))
                        scores(s, 0)
                    if s.has(1):
                        pe.wait_ge(o_done, s.item(1) + 1)
                        flat = o_sb[:, :, :].rearrange("p h d -> p (h d)")
                        transposes(s, "o", [flat[:, P * c:P * c + P] for c in range(KC)])
                    if s.has(-1):
                        scores(s, 1)
                walk(pe, FIRST_A, LAST_A, LOOP_A, NB, step)

            @block.vector
            def _(dve):
                dve.memset(k_t[:, :, :, :].bitcast(F32), 0.0).then_inc(consts_set, 1)
                dve.memset(psum_m[0][:, :], 0.0).then_inc(consts_set, 1)
                dve.memset(ones_bf[:, :], 1.0).then_inc(consts_set, 1)
                dve.wait_ge(consts_in, CONSTS_IN)
                dve.tensor_copy(before[:, :], const("before")).then_inc(consts_set, 1)
                dve.tensor_copy(taken[:, :], const("taken_first")).then_inc(consts_set, 1)
                split, rest, kept = sem("split"), o_sb[:, :, :].rearrange("p h d -> p (h d)"), xr_sb[1][:, :]
                dve.tensor_copy(b_proj_parts[:, :], b_proj_sb[:, :]).then_inc(split, 1)
                dve.wait_ge(split, 1)
                dve.tensor_tensor(rest, b_proj_sb[:, :], b_proj_parts[:, :], ALU.subtract).then_inc(split, 1)
                dve.tensor_scalar(kept, b_proj_parts[:, :], const("part0"), None, ALU.mult).then_inc(split, 1)
                dve.wait_ge(split, 3)
                dve.tensor_copy(b_proj_parts[:, :], rest).then_inc(split, 1)
                dve.wait_ge(split, 4)
                dve.scalar_tensor_tensor(out=kept, in0=b_proj_parts[:, :], scalar=const("part1"), in1=kept,
                                         op0=ALU.mult, op1=ALU.add).then_inc(split, 1)
                dve.tensor_tensor(rest, rest, b_proj_parts[:, :], ALU.subtract).then_inc(split, 1)
                dve.wait_ge(split, 6)
                dve.scalar_tensor_tensor(out=kept, in0=rest, scalar=const("part2"), in1=kept,
                                         op0=ALU.mult, op1=ALU.add).then_inc(split, 1)
                dve.wait_ge(split, 7)
                dve.tensor_copy(b_proj_parts[:, :], kept).then_inc(consts_set, 1)
                dve.wait_ge(consts_set, CONSTS_SET)

                def largest(s, half):
                    b = s.item(0)
                    dve.wait_ge(scores_done[half], b + 1)
                    if s.has(0, 1):
                        dve.wait_ge(shifted_done[half], b)
                    dve.tensor_reduce(smax[:, 8 * half:8 * half + 8], psum_s[half][:, :, :], AX.X, ALU.max).then_inc(row_max, 1)

                def shift(s, half):
                    b = s.item(0)
                    dve.wait_ge(row_max, 2 * b + half + 1)
                    if s.has(0, 1):
                        dve.wait_ge(ring_full, (s.ring("p3") if half else s.ring("p1", 1)) + 1)
                    dve.tensor_tensor(shifted[half][:, :, :], psum_s[half][:, :, :],
                                      repeat_last(smax[:, 8 * half:8 * half + 8], P), ALU.subtract).then_inc(shifted_done[half], 1)

                def step(s):
                    small = psum_m[1][:, SMALL:SMALL + 2 * E]
                    n0, n1, n2, n4, n5, nw = (s.has(lag) for lag in (0, 1, 2, 4, 5, -4))
                    b1_, b2_, b4, b5, bw = (s.item(lag) for lag in (1, 2, 4, 5, -4))
                    if n0:
                        largest(s, 0)
                    if nw:
                        dve.wait_ge(x_in[s.side(-4, 4)], 16 * (s.turn(-4, 4) + 1))
                        if s.has(-4, 1):
                            dve.wait_ge(stats1, CHAIN * bw)
                        dve.bn_stats(st1[:, :], x_sb[s.side(-4, 4)][:, :]).then_inc(stats1, 1)
                    if n0:
                        shift(s, 0)
                    if n2:
                        r2 = s.side(2, 4)
                        dve.wait_ge(proj_done, b2_ + 1)
                        dve.wait_ge(xr_in[s.side(2)], 16 * (s.turn(2) + 1))
                        if s.has(2, 4):
                            dve.wait_ge(row_out[r2], 16 * s.turn(2, 4))
                        dve.tensor_tensor(row[r2][:, 0:D], psum_m[1][:, 0:D], xr_sb[s.side(2)][:, :], ALU.add).then_inc(x2_done, 1)
                    if n4:
                        dve.wait_ge(logits_done, b4 + 1)
                    if n5:
                        h5 = hot[s.side(5)][:, :]
                        dve.wait_ge(rank_done, b5 + 1)
                        if s.has(5, 1):
                            dve.wait_ge(place_done, b5)
                        dve.tensor_tensor_reduce(spot_x[:, :], small[:, 0:E], h5, 1.0, 0.0, ALU.mult, ALU.add,
                                                 spot_f[:, :]).then_inc(place, 1)
                    if n4:
                        if s.has(4, 1):
                            dve.wait_ge(choice, 3 * b4)
                            dve.wait_ge(hot_done, b4)
                        dve.tensor_tensor(logits[:, :], small[:, E:2 * E], b_r_sb[:, :], ALU.add).then_inc(logits_read, 1)
                    if n2:
                        dve.wait_ge(x2_done, b2_ + 1)
                        if s.has(2, 1):
                            dve.wait_ge(stats2, CHAIN * b2_)
                        dve.bn_stats(st2[:, :], row[r2][:, 0:D]).then_inc(stats2, 1)
                    if n4:
                        dve.wait_ge(logits_read, b4 + 1)
                    if n5:
                        dve.tensor_tensor(taken[:, :], taken[:, :], h5, ALU.add).then_inc(taken_done, 1)
                    if n4:
                        dve.max(top[:, :], logits[:, :]).then_inc(choice, 1)
                        dve.wait_ge(choice, 3 * b4 + 1)
                    if n5:
                        dve.wait_ge(place, b5 + 1)
                        dve.tensor_scalar(spot_i[s.side(5, 4)][:, :], spot_f[:, :], float(E // 2 * REGION), None, ALU.add).then_inc(place_done, 1)
                    if n4:
                        dve.max_index(top_at[:, :], top[:, :], logits[:, :]).then_inc(choice, 1)
                    if nw:
                        dve.wait_ge(stats1, CHAIN * bw + 1)
                        if s.has(-4, 2):
                            dve.wait_ge(shift1, bw - 1)
                    if n2:
                        dve.wait_ge(stats2, CHAIN * b2_ + 1)
                        if s.has(2, 2):
                            dve.wait_ge(shift2, b2_ - 1)
                    if n0:
                        largest(s, 1)
                    if n4:
                        dve.wait_ge(choice, 3 * b4 + 2)
                        dve.tensor_copy(top_f[:, :], top_at[:, 0:1]).then_inc(choice, 1)
                    if n2:
                        dve.bn_aggr(mv2[s.side(2)][:, :], st2[:, :]).then_inc(stats2, 1)
                    if nw:
                        dve.bn_aggr(mv1[s.side(-4)][:, :], st1[:, :]).then_inc(stats1, 1)
                    if n4:
                        dve.wait_ge(choice, 3 * b4 + 3)
                        dve.tensor_scalar(hot[s.side(4)][:, :], const("expert"), top_f[:, 0:1], None, ALU.is_equal).then_inc(hot_done, 1)
                    if n2:
                        dve.wait_ge(stats2, CHAIN * b2_ + 2)
                        dve.tensor_scalar(ve2[s.side(2)][:, :], mv2[s.side(2)][:, 1:2], EPS, None, ALU.add).then_inc(stats2, 1)
                    if n1:
                        sums = psum_m[1][:, :].rearrange("p (h e) -> p h e", h=H)
                        dve.wait_ge(back_done, b1_ + 1)
                        if s.has(1, 1):
                            dve.wait_ge(o_done, b1_)
                        dve.reciprocal(recip[:, :], sums[:, :, DH]).then_inc(recip_done, 1)
                    if nw:
                        dve.wait_ge(stats1, CHAIN * bw + 2)
                        dve.tensor_scalar(ve1[s.side(-4)][:, :], mv1[s.side(-4)][:, 1:2], EPS, None, ALU.add).then_inc(stats1, 1)
                    if n1:
                        dve.wait_ge(recip_done, b1_ + 1)
                        if s.has(1, 1):
                            dve.wait_ge(ring_full, s.ring("o", 1) + 1)
                        dve.tensor_tensor(o_sb[:, :, :], sums[:, :, 0:DH], repeat_last(recip[:, :], DH), ALU.mult).then_inc(o_done, 1)
                    if n0:
                        shift(s, 1)
                walk(dve, FIRST_A, LAST_A, LOOP_A, NB, step)

        with ExitStack() as f:
            b2_sb = sb("b2_sb", [P, E, D], F32, f)
            w_now = [sb(f"w_now{i}", [P, KC, F], F32, f) for i in range(2)]
            b1_now = [sb(f"b1_now{i}", [P, FC], F32, f) for i in range(2)]
            t_in = [sb(f"t_in{i}", [P, ROW], F32, f) for i in range(4)]
            t_res = [sb(f"t_res{i}", [P, D + 1], F32, f) for i in range(2)]
            t_id = [sb(f"t_id{i}", [P, 1], U32, f) for i in range(2)]
            t_n = [sb(f"t_n{i}", [P, D], F32, f) for i in range(2)]
            t_nt = [sb(f"t_nt{i}", [P, KC, P], F32, f) for i in range(2)]
            hid = [sb(f"hid{i}", [P, FC, P], F32, f) for i in range(2)]
            t_out = [sb(f"t_out{i}", [P, D], F32, f) for i in range(2)]
            st = sb("st", [P, 6], F32, f)
            mv = sb("mv", [P, 2], F32, f)
            ve = sb("ve", [P, 1], F32, f)
            rs = sb("rs", [P, 1], F32, f)
            count = sb("count", [P, E], F32, f)
            pad_f = sb("pad_f", [P, E], F32, f)
            pad_i = [sb(f"pad_i{e}", [P, 1], U32, f) for e in range(E)]
            over = sb("over", [P, E, TOK // P], F32, f)
            tiles_of = sb("tiles_of", [P, E], F32, f)
            tiles_to = sb("tiles_to", [P, E], F32, f)
            tiles_at = sb("tiles_at", [P, E], F32, f)
            region_less = sb("region_less", [P, E], F32, f)
            past = sb("past", [P, TILES, E], F32, f)
            expert_f = sb("expert_f", [P, TILES], F32, f)
            is_expert = sb("is_expert", [P, TILES, E], F32, f)
            row_part = sb("row_part", [P, TILES, E], F32, f)
            row_f = sb("row_f", [P, TILES], F32, f)
            row_g = sb("row_g", [P, TILES], F32, f)
            row_h = sb("row_h", [P, TILES], F32, f)
            row_k = sb("row_k", [P, TILES], F32, f)
            tile_row = sb("tile_row", [P, TILES], I32, f)
            tile_expert = sb("tile_expert", [P, TILES], I32, f)

            counted, plan, pads_placed, pads_out, tables = (
                sem("counted"), sem("plan"), sem("pads_placed"), sem("pads_out"), sem("tables"))
            b2_in = sem("b2_in")
            t_loaded, t_done = [sem(f"t_loaded{i}") for i in range(4)], sems("t_done")
            t_root = sem("t_root")
            t_ln, t_kept, t_turned, t_turned_read = sem("t_ln"), sem("t_kept"), sem("t_turned"), sem("t_turned_read")
            w1_set, b1_set = sem("w1_set"), sem("b1_set")
            hid_done, hid_read, y_done, y_read = sem("hid_done"), sem("hid_read"), sem("y_done"), sem("y_read")

            block = f.enter_context(nc.Block())

            @block.sync
            def _(sp):
                sp.dma_start(b2_sb[:, :, :].rearrange("p e d -> p (e d)"), spread(b2, 0, P)).then_inc(b2_in, 16)
                sp.wait_ge(pads_out, 16 * E)
                sp.wait_ge(tables, 2)

                def step(s):
                    if s.has(-3):
                        p = s.side(-3, 4)
                        row = sp.value_load(tile_row[0:1, bass.ds(s.item(-3), 1)], min_val=0, max_val=SPARE)
                        if s.has(-3, 4):
                            sp.wait_ge(t_kept, 2 * (s.item(-3) - 3))
                        sp.dma_start(t_in[p][:, :], routed[bass.ds(row, P), :]).then_inc(t_loaded[p], 16)
                walk(sp, FIRST_F, LAST_F, LOOP_F, TILES, step)

            @block.gpsimd
            def _(pool):
                pool.wait_ge(pads_placed, E)
                for e in range(E):
                    pool.indirect_dma_start(
                        out=routed, out_offset=bass.IndirectOffsetOnAxis(ap=pad_i[e][:, 0:1], axis=0),
                        in_=pad[:, :], in_offset=None).then_inc(pads_out, 16)

                def step(s):
                    if s.has(2):
                        pool.wait_ge(y_read, 2 * (s.item(2) + 1))
                    if s.has(-2):
                        pool.wait_ge(t_ln, (CHAIN + 1) * s.item(-2) + CHAIN)
                        pool.tensor_tensor(rs[:, :], ve[:, :], const("power"), ALU.pow).then_inc(t_root, 1)
                    if s.has(2):
                        p = s.side(2)
                        pool.indirect_dma_start(
                            out=out_rows, out_offset=bass.IndirectOffsetOnAxis(ap=t_id[p][:, 0:1], axis=0),
                            in_=t_out[p][:, :], in_offset=None, bounds_check=TOK - 1, oob_is_err=False).then_inc(t_done[p], 16)
                walk(pool, FIRST_F, LAST_F, LOOP_F, TILES, step)
                for p in range(2):
                    pool.wait_ge(t_done[p], 16 * ((TILES + 1 - p) // 2))

            @block.scalar
            def _(act):
                def step(s):
                    if s.has(-1):
                        p = s.side(-1)
                        act.wait_ge(t_turned, s.item(-1) + 1)
                        if s.has(-1, 2):
                            act.wait_ge(hid_done, 2 * (s.item(-1) - 1))
                        act.activation(t_nt[p][:, :, :], psum_r[p][:, 0:D].rearrange("p (c t) -> p c t", c=KC), ACT.Copy).then_inc(t_turned_read, 1)
                    if s.has(0):
                        p = s.side(0)
                        act.wait_ge(b1_set, s.item(0) + 1)
                        if s.has(0, 2):
                            act.wait_ge(y_done, s.item(0) - 1)
                        for c in range(FC):
                            if c % 4 == 0:
                                act.wait_ge(hid_done, 2 * s.item(0) + c // 4 + 1)
                            act.activation(hid[p][:, c, :], psum_s[p][:, c, :], ACT.Relu, bias=b1_now[p][:, c:c + 1]).then_inc(hid_read, 1)
                walk(act, FIRST_F, LAST_F, LOOP_F, TILES, step)

            @block.tensor
            def _(pe):
                pe.matmul(psum_m[0][:, 0:E], ones_bf[:, :], taken[:, :], start=True, stop=True).then_inc(counted, 1)

                pe.wait_ge(tables, 2)
                pe.wait_ge(experts_in, 16 * NB)

                def step(s):
                    if s.has(-1):
                        b, p = s.item(-1), s.side(-1)
                        pe.wait_ge(t_ln, (CHAIN + 1) * (b + 1))
                        if s.has(-1, 2):
                            pe.wait_ge(t_turned_read, b - 1)
                        for c in range(KC):
                            last = pe.transpose(psum_r[p][:, P * c:P * c + P], t_n[p][:, P * c:P * c + P], ident)
                        last.then_inc(t_turned, 1)
                    if s.has(1):
                        b, p = s.item(1), s.side(1)
                        e = pe.value_load(tile_expert[0:1, bass.ds(b, 1)], min_val=0, max_val=E - 1)
                        if s.has(1, 2):
                            pe.wait_ge(y_read, 2 * (b - 1))
                        else:
                            pe.wait_ge(plan, 1)
                        for c in range(FC):
                            if c % 4 == 0:
                                pe.wait_ge(hid_read, FC * b + c + 4)
                            w2 = w_sb[:, bass.ds(4 * e + 2 + c // 4, 1), D * (c % 4):D * (c % 4 + 1)].rearrange("p a d -> p (a d)")
                            last = pe.matmul(psum_m[p][:, 0:D], hid[p][:, c, :], w2, start=(c == 0), stop=(c == FC - 1))
                        last.then_inc(y_done, 1)
                    if s.has(0):
                        b, p = s.item(0), s.side(0)
                        pe.wait_ge(t_turned_read, b + 1)
                        pe.wait_ge(w1_set, b + 1)
                        if s.has(0, 2):
                            pe.wait_ge(hid_read, FC * (b - 1))
                        for c in range(FC):
                            for k in range(KC):
                                last = pe.matmul(psum_s[p][:, c, :], w_now[p][:, k, P * c:P * c + P], t_nt[p][:, k, :],
                                                 start=(k == 0), stop=(k == KC - 1))
                            if c % 4 == 3:
                                last.then_inc(hid_done, 1)
                walk(pe, FIRST_F, LAST_F, LOOP_F, TILES, step)

            @block.vector
            def _(dve):
                at = [0]

                def then(ins):
                    ins.then_inc(plan, 1)
                    at[0] += 1
                    dve.wait_ge(plan, at[0])

                dve.wait_ge(counted, 1)
                then(dve.tensor_tensor(count[:, :], psum_m[0][:, 0:E], const("count_back"), ALU.add))
                then(dve.tensor_tensor(pad_f[:, :], count[:, :], const("pad_row"), ALU.add))
                for e in range(E):
                    dve.tensor_copy(pad_i[e][:, :], pad_f[:, e:e + 1]).then_inc(pads_placed, 1)
                then(dve.tensor_tensor(over[:, :, :], repeat_last(count[:, :], TOK // P), spread(const("full_rows"), 1, E), ALU.is_gt))
                then(dve.tensor_reduce(tiles_of[:, :], over[:, :, :], AX.X, ALU.add))
                then(dve.tensor_tensor_scan(tiles_to[:, :], tiles_of[:, :], tiles_of[:, :], 0.0, ALU.add, ALU.bypass))
                then(dve.tensor_tensor(tiles_at[:, :], tiles_to[:, :], tiles_of[:, :], ALU.subtract))
                then(dve.scalar_tensor_tensor(out=region_less[:, :], in0=tiles_at[:, :], scalar=-float(P), in1=const("region"),
                                              op0=ALU.mult, op1=ALU.add))
                then(dve.tensor_tensor(past[:, :, :], spread(tiles_to[:, :], 1, TILES), repeat_last(const("tile"), E), ALU.is_le))
                then(dve.tensor_reduce(expert_f[:, :], past[:, :, :], AX.X, ALU.add))
                then(dve.tensor_tensor(is_expert[:, :, :], repeat_last(expert_f[:, :], E), spread(const("expert"), 1, TILES), ALU.is_equal))
                then(dve.tensor_tensor(row_part[:, :, :], is_expert[:, :, :], spread(region_less[:, :], 1, TILES), ALU.mult))
                then(dve.tensor_reduce(row_f[:, :], row_part[:, :, :], AX.X, ALU.add))
                then(dve.tensor_tensor(row_g[:, :], row_f[:, :], const("tile_row"), ALU.add))
                then(dve.tensor_scalar(row_h[:, :], expert_f[:, :], float(E), float(SPARE), ALU.is_ge, ALU.mult))
                then(dve.tensor_tensor(row_k[:, :], row_g[:, :], row_h[:, :], ALU.add))
                dve.tensor_scalar(tile_row[:, :], row_k[:, :], float(SPARE), None, ALU.min).then_inc(tables, 1)
                dve.tensor_scalar(tile_expert[:, :], expert_f[:, :], float(E - 1), None, ALU.min).then_inc(tables, 1)
                dve.wait_ge(tables, 2)
                dve.wait_ge(experts_in, 16 * NB)
                dve.wait_ge(b2_in, 16)

                def step(s):
                    if s.has(-2):
                        b, p, p4 = s.item(-2), s.side(-2), s.side(-2, 4)
                        base = (CHAIN + 1) * b
                        dve.wait_ge(t_loaded[p4], 16 * (s.turn(-2, 4) + 1))
                        if s.has(-2, 1):
                            dve.wait_ge(t_ln, base)
                        dve.bn_stats(st[:, :], t_in[p4][:, 0:D]).then_inc(t_ln, 1)
                        dve.wait_ge(t_ln, base + 1)
                    if s.has(-1):
                        q = s.side(-1)
                        e = dve.value_load(tile_expert[0:1, bass.ds(s.item(-1), 1)], min_val=0, max_val=E - 1)
                        if s.has(-1, 2):
                            dve.wait_ge(hid_done, 2 * (s.item(-1) - 1))
                        dve.tensor_copy(w_now[q][:, :, :], w_sb[:, bass.ds(4 * e, 2), :]).then_inc(w1_set, 1)
                    if s.has(-2):
                        dve.bn_aggr(mv[:, :], st[:, :]).then_inc(t_ln, 1)
                        dve.wait_ge(t_ln, base + 2)
                        dve.tensor_scalar(ve[:, :], mv[:, 1:2], EPS, None, ALU.add).then_inc(t_ln, 1)
                    if s.has(0):
                        r, r4 = s.side(0), s.side(0, 4)
                        e0 = dve.value_load(tile_expert[0:1, bass.ds(s.item(0), 1)], min_val=0, max_val=E - 1)
                        if s.has(0, 2):
                            dve.wait_ge(y_read, 2 * (s.item(0) - 1))
                        dve.tensor_tensor(t_res[r][:, 0:D], t_in[r4][:, 0:D], b2_sb[:, bass.ds(e0, 1), :].rearrange("p a d -> p (a d)"),
                                          ALU.add).then_inc(t_kept, 1)
                        dve.tensor_copy(t_res[r][:, D:D + 1], t_in[r4][:, D:D + 1]).then_inc(t_kept, 1)
                    if s.has(-2):
                        dve.wait_ge(t_root, b + 1)
                        if s.has(-2, 2):
                            dve.wait_ge(t_turned, b - 1)
                        dve.tensor_scalar(t_n[p][:, :], t_in[p4][:, 0:D], mv[:, 0:1], rs[:, 0:1], ALU.subtract, ALU.mult).then_inc(t_ln, 1)
                    if s.has(1):
                        q = s.side(1)
                        dve.wait_ge(y_done, s.item(1) + 1)
                        if s.has(1, 2):
                            dve.wait_ge(t_done[q], 16 * s.turn(1))
                        dve.wait_ge(t_kept, 2 * (s.item(1) + 1))
                        dve.tensor_tensor(t_out[q][:, :], psum_m[q][:, 0:D], t_res[q][:, 0:D], ALU.add).then_inc(y_read, 1)
                        dve.tensor_copy(t_id[q][:, :], t_res[q][:, D:D + 1]).then_inc(y_read, 1)
                    if s.has(-1):
                        if s.has(-1, 2):
                            dve.wait_ge(hid_read, FC * (s.item(-1) - 1))
                        dve.tensor_copy(b1_now[s.side(-1)][:, :], b1_sb[:, bass.ds(e, 1), :].rearrange("p a c -> p (a c)")).then_inc(b1_set, 1)
                walk(dve, FIRST_F, LAST_F, LOOP_F, TILES, step)


def constants():
    import numpy as np
    t = np.zeros((P, CONST_WIDTH), np.float32)

    def put(name, value):
        a, b = CONST_COLS[name]
        t[:, a:b] = value
    lane = np.arange(P)
    put("ident", np.eye(P))
    put("before", lane[:, None] < lane[None, :])
    put("region", REGION * np.arange(E)[None])
    put("taken_first", REGION // P * (np.arange(E)[None] - E // 2))
    put("count_back", REGION * (E // 2 - np.arange(E)[None]))
    put("pad_row", REGION * np.arange(E)[None] + lane[:, None])
    put("expert", np.arange(E)[None])
    put("full_rows", P * np.arange(TOK // P)[None])
    put("tile", np.arange(TILES)[None])
    put("tile_row", P * np.arange(TILES)[None])
    put("minus_hi", -(lane // 32 % 2)[:, None])
    put("lane", lane[:, None])
    put("power", -0.5)
    put("round", UNROLL * P)
    for part in range(3):
        put(f"part{part}", (lane == part)[:, None])
    return t


def kernel(x, ctx_1024, L0_xattn_w_proj, L0_xattn_b_proj, L0_ffn_Wr, L0_ffn_br, L0_ffn_W1, L0_ffn_b1, L0_ffn_W2, L0_ffn_b2):
    import numpy as np
    import concourse.bacc as bacc
    from concourse.bass_utils import run_bass_kernel_spmd

    x = np.asarray(x)
    ctx = np.asarray(ctx_1024)
    heads = ctx.reshape(NB, P, PAIRS, 2, DH).transpose(0, 3, 4, 2, 1)
    w1 = np.asarray(L0_ffn_W1).transpose(0, 2, 1).reshape(E, 2, P, F)
    w2 = np.asarray(L0_ffn_W2).transpose(0, 2, 1).reshape(E, 2, FC // 2, P, D).transpose(0, 1, 3, 2, 4).reshape(E, 2, P, F)
    arrays = {
        "x": x,
        "ctx_rows": np.concatenate([ctx.reshape(TOK, H, DH), np.ones((TOK, H, 1), ctx.dtype)], axis=2).reshape(TOK, H * (DH + 1)),
        "ctx_heads": heads,
        "w_proj_t": np.asarray(L0_xattn_w_proj).T,
        "b_proj": np.asarray(L0_xattn_b_proj).reshape(1, D),
        "wr_t": np.asarray(L0_ffn_Wr).T,
        "b_r": np.asarray(L0_ffn_br).reshape(1, E),
        "experts": np.concatenate([w1, w2], axis=1).reshape(4 * E, P, F),
        "b1_cols": np.asarray(L0_ffn_b1).reshape(E, FC, P).transpose(2, 0, 1),
        "b2": np.asarray(L0_ffn_b2).reshape(1, E * D),
        "consts": constants(),
    }
    arrays = {f"in_{k}": np.ascontiguousarray(v) for k, v in arrays.items()}
    nc = bacc.Bacc("TRN2", target_bir_lowering=False, num_devices=1)
    args = [nc.dram_tensor(k, v.shape, mybir.dt.from_np(v.dtype), kind="ExternalInput").ap() for k, v in arrays.items()]
    out = nc.dram_tensor("out", (NB, P, D), F32, kind="ExternalOutput").ap()
    build(nc, *args, out)
    r = run_bass_kernel_spmd(nc, [arrays], core_ids=[0])
    return r.results[0]["out"]
```

```python
from contextlib import ExitStack

import numpy as np

import concourse.bass as bass
from concourse import mybir

P = 128
D = 256
H = 16
DH = D // H
PAIRS = H // 2
NB = 32
TOK = NB * P
E = 8
F = 1024
KC = D // P
FC = F // P
TILES = TOK // P + E - 1
REGION = TOK + P
SPARE = E * REGION
ROW = D + 16
NOWHERE = 1.0e6
SCALE = 1.0 / DH ** 0.5
EPS = 1e-5

F32 = mybir.dt.float32
F32R = mybir.dt.float32r
BF16 = mybir.dt.bfloat16
I32 = mybir.dt.int32
U32 = mybir.dt.uint32
ALU = mybir.AluOpType
ACT = mybir.ActivationFunctionType
AX = mybir.AxisListType

CONST_COLS = {}
CONST_WIDTH = 0
for _name, _n in (("ident", P), ("before", P), ("region", E), ("taken_first", E), ("count_back", E), ("expert", E),
                  ("full_rows", TOK // P), ("tile", TILES), ("tile_row", TILES), ("minus_hi", 1), ("lane", 1), ("power", 1), ("round", 1),
                  ("part0", 1), ("part1", 1), ("part2", 1)):
    CONST_COLS[_name] = (CONST_WIDTH, CONST_WIDTH + _n)
    CONST_WIDTH += _n

RING = (("p0", 0), ("p1", 0), ("q_a", -1), ("q_b", -1), ("n", 3), ("p2", 0), ("p3", 0), ("o", 1))
UNROLL = 4
FIRST_A, LAST_A = -5, NB + 4
LOOP_A = (2, 7)
FIRST_F, LAST_F = -3, TILES + 1
LOOP_F = (1, 9)


def uses_before(step):
    return sum(1 for s in range(FIRST_A, step) for _, lag in RING if 0 <= s - lag < NB)


STEADY = uses_before(UNROLL * LOOP_A[0]) - len(RING) * UNROLL * LOOP_A[0]


class Step:

    def __init__(self, round_, place, count):
        self.round, self.place, self.count = round_, place, count
        self.fixed = isinstance(round_, int)
        self.number = UNROLL * round_ + place

    def has(self, lag, least=0):
        return not self.fixed or least <= self.number - lag < self.count

    def item(self, lag):
        return self.number - lag

    def side(self, lag, n=2):
        return (self.place - lag) % n

    def turn(self, lag, n=2):
        return UNROLL // n * self.round + (self.place - lag) // n

    def ring(self, name, back=0):
        at = [n for n, _ in RING].index(name)
        if not self.fixed:
            return self.number * len(RING) + (STEADY - back * len(RING) + at)
        s = self.number - back
        return uses_before(s) + sum(1 for _, lag in RING[:at] if 0 <= s - lag < NB)

    def bank(self, name):
        if self.fixed:
            return self.ring(name) % 2
        return (STEADY + [n for n, _ in RING].index(name)) % 2


def walk(engine, first, last, loop, count, body):
    for s in range(first, UNROLL * loop[0]):
        body(Step(s // UNROLL, s % UNROLL, count))
    with engine.Fori(loop[0], loop[1]) as round_:
        for place in range(UNROLL):
            body(Step(round_, place, count))
    for s in range(UNROLL * loop[1], last + 1):
        body(Step(s // UNROLL, s % UNROLL, count))


def spread(ap, axis, n):
    names = [f"a{i}" for i in range(len(ap.shape))]
    inner = names[:axis] + [f"(o {names[axis]})"] + names[axis + 1:]
    out = names[:axis] + ["o", names[axis]] + names[axis + 1:]
    v = ap.rearrange(" ".join(inner) + " -> " + " ".join(out), o=1)
    shape = list(v.shape)
    shape[axis] = n
    return v.to_broadcast(shape)


def repeat_last(ap, n):
    names = [f"a{i}" for i in range(len(ap.shape))]
    v = ap.rearrange(" ".join(names[:-1] + [f"({names[-1]} o)"]) + " -> " + " ".join(names + ["o"]), o=1)
    return v.to_broadcast(list(ap.shape) + [n])


def build(nc, x, ctx_rows, ctx_heads, w_proj_t, b_proj, wr_t, b_r, experts, b1_cols, b2, consts, out):
    routed = nc.dram_tensor("routed", (SPARE + P, ROW), F32).ap()
    x_rows = x.rearrange("b t d -> (b t) d")
    out_rows = out.rearrange("b t d -> (b t) d")

    with ExitStack() as ctx:
        def sb(name, shape, dt, where=None):
            return (where or ctx).enter_context(nc.sbuf_tensor(name, shape, dt))

        def sem(name):
            return ctx.enter_context(nc.semaphore(name))

        def sems(name):
            return [sem(f"{name}{i}") for i in range(2)]

        psum_s = [ctx.enter_context(nc.psum_tensor(f"scores{h}", [P, PAIRS, P], F32)) for h in range(2)]
        psum_r = [ctx.enter_context(nc.psum_tensor(f"transfer{i}", [P, 512], F32)) for i in range(2)]
        psum_m = [ctx.enter_context(nc.psum_tensor(f"sums{i}", [P, 512], F32)) for i in range(2)]

        cst = sb("cst", [P, CONST_WIDTH], F32)

        def const(name):
            a, b = CONST_COLS[name]
            return cst[:, a:b]

        ident = const("ident")
        before = sb("before", [P, P], BF16)
        ones_bf = sb("ones_bf", [P, P], BF16)
        b_proj_parts = sb("b_proj_parts", [P, D], BF16)
        w_proj_sb = sb("w_proj_sb", [P, KC, D], F32)
        wr_sb = sb("wr_sb", [P, KC, E], F32)
        b1_sb = sb("b1_sb", [P, E, FC], F32)
        w_sb = sb("w_sb", [P, 4 * E, F], F32)
        taken = sb("taken", [P, E], BF16)
        pad = sb("pad", [P, ROW], F32)
        pad_row = sb("pad_row", [P, E], I32)
        tile_row = sb("tile_row", [P, TILES], I32)
        tile_expert = sb("tile_expert", [P, TILES], I32)

        cst_in = sem("cst_in")
        consts_in = sem("consts_in")
        consts_set = sem("consts_set")
        experts_in = sem("experts_in")
        spare_written = sem("spare_written")
        counted, plan, pads_placed, pads_out, tables = (
            sem("counted"), sem("plan"), sem("pads_placed"), sem("pads_out"), sem("tables"))
        x_in, row_out = ([sem(f"{n}{i}") for i in range(4)] for n in ("x_in", "row_out"))
        k_in, v_in, xr_in = sems("k_in"), sems("v_in"), sems("xr_in")
        stats1, root1, shift1, norm1 = sem("stats1"), sem("root1"), sem("shift1"), sem("norm1")
        q_lo = sem("q_lo")
        k_neg, k_split, k_ready = sem("k_neg"), sem("k_split"), sem("k_ready")
        scores_done = sems("scores_done")
        row_max = sem("row_max")
        shifted_done = sems("shifted_done")
        ring_full, ring_read = sem("ring_full"), sem("ring_read")
        pv_done, pv_read, back_done = sem("pv_done"), sem("pv_read"), sem("back_done")
        recip_done, o_done = sem("recip_done"), sem("o_done")
        proj_done, x2_done = sem("proj_done"), sem("x2_done")
        stats2, root2, shift2, norm2 = sem("stats2"), sem("root2"), sem("shift2"), sem("norm2")
        logits_done, logits_read = sem("logits_done"), sem("logits_read")
        choice, hot_done = sem("choice"), sem("hot_done")
        rank_done, taken_done, place, place_done = sem("rank_done"), sem("taken_done"), sem("place"), sem("place_done")
        number_set = sem("number_set")

        CHAIN = 3
        CONSTS_IN = 16 * 5
        CONSTS_SET = 7
        NUMBERS = 9
        SMALL = 384
        QUAD = 4

        a = ExitStack()
        with a:
            b_proj_sb = sb("b_proj_sb", [P, D], F32, a)
            b_r_sb = sb("b_r_sb", [P, E], F32, a)
            x_sb = [sb(f"x_sb{i}", [P, D], F32, a) for i in range(4)]
            xn = sb("xn", [P, D], F32, a)
            q_parts = [sb(f"q_parts{i}", [P, H, 2, 2, DH], F32, a) for i in range(2)]
            q_t = sb("q_t", [P, PAIRS, P], F32R, a)
            k_raw = [sb(f"k_raw{i}", [P, PAIRS, P], F32, a) for i in range(2)]
            k_parts = [sb(f"k_parts{i}", [P, PAIRS, P], F32R, a) for i in range(2)]
            k_t = sb("k_t", [P, PAIRS, 2, P], F32R, a)
            shifted = [sb(f"shifted{i}", [P, PAIRS, P], F32, a) for i in range(2)]
            p_t = sb("p_t", [P, H, P], F32, a)
            v_one = [sb(f"v_one{i}", [P, H, DH + 1], F32, a) for i in range(2)]
            xr_sb = [sb(f"xr_sb{i}", [P, D], F32, a) for i in range(2)]
            pv_t = sb("pv_t", [P, H // QUAD, P], F32, a)
            o_sb = sb("o_sb", [P, H, DH], F32, a)
            o_t = sb("o_t", [P, KC, P], F32, a)
            row = [sb(f"row{i}", [P, ROW], F32, a) for i in range(4)]
            x2n = sb("x2n", [P, D], F32, a)
            x2n_t = sb("x2n_t", [P, KC, P], F32, a)
            st1, st2 = sb("st1", [P, 6], F32, a), sb("st2", [P, 6], F32, a)
            mv1, mv2 = ([sb(f"mv{n}{i}", [P, 2], F32, a) for i in range(2)] for n in (1, 2))
            ve1, ve2 = ([sb(f"ve{n}{i}", [P, 1], F32, a) for i in range(2)] for n in (1, 2))
            rs1, rs2 = ([sb(f"rs{n}{i}", [P, 1], F32, a) for i in range(2)] for n in (1, 2))
            nm1, nm2 = ([sb(f"nm{n}{i}", [P, 1], F32, a) for i in range(2)] for n in (1, 2))
            smax = sb("smax", [P, H], F32, a)
            recip = sb("recip", [P, H], F32, a)
            logits = sb("logits", [P, E], F32, a)
            top = sb("top", [P, E], F32, a)
            top_at = sb("top_at", [P, E], U32, a)
            top_f = sb("top_f", [P, 1], F32, a)
            hot = [sb(f"hot{i}", [P, E], BF16, a) for i in range(2)]
            spot_x = sb("spot_x", [P, E], F32, a)
            spot_f = sb("spot_f", [P, 1], F32, a)
            spot_i = [sb(f"spot_i{i}", [P, 1], U32, a) for i in range(4)]

            def pad_experts(queue, which):
                queue.wait_ge(pads_placed, 1)
                for e in which:
                    first = queue.value_load(pad_row[0:1, e:e + 1], min_val=0, max_val=SPARE)
                    queue.dma_start(routed[bass.ds(first, P), :], pad[:, :]).then_inc(pads_out, 16)

            block = a.enter_context(nc.Block())

            @block.sync
            def _(sp):
                def step(s):
                    if s.has(-1, 1):
                        sp.wait_ge(scores_done[1], s.item(-1))
                    elif s.has(-1):
                        sp.wait_ge(consts_set, CONSTS_SET)
                    if s.has(-5):
                        p = s.side(-5, 4)
                        if s.fixed and s.has(-5, 4):
                            sp.wait_ge(norm1, s.item(-5) - 3)
                        sp.dma_start(x_sb[p][:, :], x_rows[bass.ds(s.item(-5) * P, P), :]).then_inc(x_in[p], 16)
                        if s.fixed and s.item(-5) == 0:
                            sp.dma_start(cst[:, :], consts).then_inc(cst_in, 16)
                    if s.has(-1):
                        p = s.side(-1)
                        sp.wait_ge(k_split, s.item(-1) + 1)
                        for h in range(2):
                            sp.dma_start(k_t[64 * h:64 * h + 64, :, h, :].bitcast(F32), k_parts[p][64 * h:64 * h + 64, :, :].bitcast(F32)).then_inc(k_ready, 16)
                        if s.has(-1, 2):
                            sp.wait_ge(pv_done, s.item(-1) - 1)
                        sp.dma_start(v_one[p][:, :, :].rearrange("p h e -> p (h e)"), ctx_rows[bass.ds(s.item(-1) * P, P), :]).then_inc(v_in[p], 16)
                    if s.has(1):
                        p = s.side(1)
                        if s.has(1, 2):
                            sp.wait_ge(x2_done, s.item(1) - 1)
                        sp.dma_start(xr_sb[p][:, :], x_rows[bass.ds(s.item(1) * P, P), :]).then_inc(xr_in[p], 16)
                    if s.has(-4):
                        p = s.side(-4)
                        if s.has(-4, 2):
                            sp.wait_ge(k_split, s.item(-4) - 1)
                        for h in range(2):
                            sp.dma_start(k_raw[p][64 * h:64 * h + 64, :, :],
                                         spread(ctx_heads[bass.ds(s.item(-4), 1), h].rearrange("b d j s -> (b d) (j s)"), 0, 4)
                                         ).then_inc(k_in[p], 16)
                    if s.has(0):
                        sp.dma_start(w_sb[:, bass.ds(s.item(0), 1), :].rearrange("p c f -> p (c f)"),
                                     experts[bass.ds(s.item(0), 1)].rearrange("c p f -> (c p) f")).then_inc(experts_in, 16)
                walk(sp, FIRST_A, LAST_A, (LOOP_A[0], LOOP_A[1] - 1), NB, step)
                sp.dma_start(routed[SPARE:SPARE + P, :], pad[:, :]).then_inc(spare_written, 16)
                pad_experts(sp, range(0, E, 2))

            @block.gpsimd
            def _(pool):
                pool.memset(pad[:, :], 0.0).then_inc(number_set, 1)
                for p in range(4):
                    pool.memset(row[p][:, D:ROW], 0.0).then_inc(number_set, 1)
                pool.wait_ge(cst_in, 16)
                pool.wait_ge(number_set, 5)
                pool.memset(pad[:, D:D + 1], NOWHERE).then_inc(consts_set, 1)
                for p in range(4):
                    pool.tensor_scalar(row[p][:, D:D + 1], const("lane"), float((p - UNROLL) * P), None, ALU.add).then_inc(number_set, 1)

                def step(s):
                    if s.has(3):
                        p = s.side(3)
                        pool.wait_ge(stats2, CHAIN * (s.item(3) + 1))
                        if s.has(3, 2):
                            pool.wait_ge(norm2, s.item(3) - 1)
                        pool.tensor_tensor(rs2[p][:, :], ve2[p][:, :], const("power"), ALU.pow).then_inc(root2, 1)
                    if s.has(-3):
                        q = s.side(-3)
                        pool.wait_ge(stats1, CHAIN * (s.item(-3) + 1))
                        if s.has(-3, 2):
                            pool.wait_ge(norm1, s.item(-3) - 1)
                        pool.tensor_tensor(rs1[q][:, :], ve1[q][:, :], const("power"), ALU.pow).then_inc(root1, 1)
                    if s.has(3):
                        pool.wait_ge(root2, s.item(3) + 1)
                    if s.has(-3):
                        pool.wait_ge(root1, s.item(-3) + 1)
                    if s.has(3):
                        r = s.side(3, 4)
                        if s.has(3, 4):
                            pool.wait_ge(row_out[r], 16 * s.turn(3, 4))
                        else:
                            pool.wait_ge(number_set, 6 + r)
                        pool.tensor_tensor(row[r][:, D:D + 1], row[r][:, D:D + 1], const("round"), ALU.add).then_inc(number_set, 1)
                        pool.tensor_scalar(nm2[p][:, :], mv2[p][:, 0:1], rs2[p][:, 0:1], -1.0, ALU.mult, ALU.mult).then_inc(shift2, 1)
                    if s.has(-3):
                        pool.tensor_scalar(nm1[q][:, :], mv1[q][:, 0:1], rs1[q][:, 0:1], -1.0, ALU.mult, ALU.mult).then_inc(shift1, 1)
                    if s.has(-2):
                        p = s.side(-2)
                        pool.wait_ge(k_neg, s.item(-2) + 1)
                        pool.tensor_tensor(k_parts[p][:, :, :], k_raw[p][:, :, :], k_parts[p][:, :, :].bitcast(F32), ALU.add
                                           ).then_inc(k_split, 1)
                        pool.wait_ge(norm1, s.item(-2) + 1)
                        lo = [q_parts[p][:, :, c, 1, :] for c in range(2)]
                        hi = [q_parts[p][:, :, c, 0, :] for c in range(2)]
                        x_heads = xn[:, :].rearrange("p (h d) -> p h d", h=H)
                        pool.tensor_tensor(lo[0], x_heads, hi[0], ALU.subtract).then_inc(q_lo, 1)
                    if s.has(5):
                        pool.wait_ge(number_set, NUMBERS + s.item(5) + 1)
                        pool.wait_ge(place_done, s.item(5) + 1)
                    if s.has(-2):
                        pool.tensor_tensor(lo[1], x_heads, hi[1], ALU.subtract).then_inc(q_lo, 1)
                    if s.has(5):
                        r = s.side(5, 4)
                        pool.indirect_dma_start(
                            out=routed, out_offset=bass.IndirectOffsetOnAxis(ap=spot_i[r][:, 0:1], axis=0),
                            in_=row[r][:, :], in_offset=None).then_inc(row_out[r], 16)
                walk(pool, FIRST_A, LAST_A, LOOP_A, NB, step)
                for p in range(4):
                    pool.wait_ge(row_out[p], 16 * (NB // 4))
                pool.wait_ge(spare_written, 16)

            @block.scalar
            def _(act):
                act.dma_start(b_proj_sb[:, :], spread(b_proj, 0, P)).then_inc(consts_in, 16)
                act.dma_start(w_proj_sb[:, :, :], w_proj_t.rearrange("(c p) n -> p c n", p=P)).then_inc(consts_in, 16)
                act.dma_start(wr_sb[:, :, :], wr_t.rearrange("(c p) n -> p c n", p=P)).then_inc(consts_in, 16)
                act.dma_start(b_r_sb[:, :], spread(b_r, 0, P)).then_inc(consts_in, 16)
                act.dma_start(b1_sb[:, :, :], b1_cols).then_inc(consts_in, 16)
                act.wait_ge(cst_in, 16)

                def read_ring(s, name, out, func, scale=1.0):
                    n = s.ring(name)
                    act.wait_ge(ring_full, n + 1)
                    src = psum_r[s.bank(name)][:, 0:out.free_size()]
                    if len(out.shape) == 3:
                        src = src.rearrange("p (c t) -> p c t", c=out.shape[1])
                    act.activation(out, src, func, scale=scale).then_inc(ring_read, 1)

                def step(s):
                    if s.has(3):
                        p, r = s.side(3), s.side(3, 4)
                        act.wait_ge(shift2, s.item(3) + 1)
                        act.activation(x2n[:, :], row[r][:, 0:D], ACT.Identity, bias=nm2[p][:, 0:1], scale=rs2[p][:, 0:1]).then_inc(norm2, 1)
                    if s.has(0):
                        for n in range(2):
                            read_ring(s, f"p{n}", p_t[:, 4 * n:4 * n + 4, :], ACT.Exp, scale=SCALE)
                    if s.has(1):
                        act.wait_ge(pv_done, s.item(1) + 1)
                        act.activation(pv_t[:, :, :], psum_m[0][:, :].rearrange("p (g t) -> p g t", t=P), ACT.Copy).then_inc(pv_read, 1)
                    if s.has(-1):
                        for n, name in enumerate(("q_a", "q_b")):
                            read_ring(s, name, q_t[:, 4 * n:4 * n + 4, :], ACT.Copy)
                    if s.has(-3):
                        p, r = s.side(-3), s.side(-3, 4)
                        act.wait_ge(shift1, s.item(-3) + 1)
                        act.activation(q_parts[p][:, :, :, 0, :].bitcast(F32R),
                                       spread(x_sb[r][:, :].rearrange("p (h d) -> p h d", h=H), 2, 2),
                                       ACT.Identity, bias=nm1[p][:, 0:1], scale=rs1[p][:, 0:1])
                    if s.has(3):
                        read_ring(s, "n", x2n_t[:, :, :], ACT.Copy)
                    if s.has(0):
                        for n in range(2, 4):
                            read_ring(s, f"p{n}", p_t[:, 4 * n:4 * n + 4, :], ACT.Exp, scale=SCALE)
                    if s.has(1):
                        read_ring(s, "o", o_t[:, :, :], ACT.Copy)
                    if s.has(-3):
                        p, r = s.side(-3), s.side(-3, 4)
                        if s.has(-3, 1):
                            act.wait_ge(q_lo, 2 * s.item(-3))
                        act.activation(xn[:, :], x_sb[r][:, :], ACT.Identity, bias=nm1[p][:, 0:1], scale=rs1[p][:, 0:1]).then_inc(norm1, 1)
                    if s.has(-3):
                        p = s.side(-3)
                        act.wait_ge(k_in[p], 32 * (s.turn(-3) + 1))
                        if s.has(-3, 2):
                            act.wait_ge(k_ready, 32 * (s.item(-3) - 1))
                        act.activation(k_parts[p][:, :, :], k_raw[p][:, :, :], ACT.Copy, scale=const("minus_hi")).then_inc(k_neg, 1)
                walk(act, FIRST_A, LAST_A, LOOP_A, NB, step)
                pad_experts(act, range(1, E, 2))

            @block.tensor
            def _(pe):
                pe.wait_ge(cst_in, 16)
                pe.wait_ge(consts_in, CONSTS_IN)
                pe.wait_ge(consts_set, CONSTS_SET)

                def transposes(s, name, parts):
                    n = s.ring(name)
                    if not s.fixed or n >= 2:
                        pe.wait_ge(ring_read, n - 1)
                    for c, part in enumerate(parts):
                        last = pe.transpose(psum_r[s.bank(name)][:, P * c:P * c + P], part, ident)
                    last.then_inc(ring_full, 1)

                def scores(s, half):
                    for j in range(PAIRS // 2):
                        pair = PAIRS // 2 * half + j
                        last = pe.matmul(psum_s[half][:, 2 * j:2 * j + 2, :], q_t[:, pair, :], k_t[:, pair, :, :],
                                         start=True, stop=True)
                    last.then_inc(scores_done[half], 1)

                def weigh(side, half):
                    for h in range(half * PAIRS, half * PAIRS + PAIRS):
                        j, g = h % QUAD, h // QUAD
                        last = pe.matmul(psum_m[0][32 * j:32 * j + DH + 1, P * g:P * g + P], v_one[side][:, h, :], p_t[:, h, :],
                                         start=True, stop=True)
                    return last

                def step(s):
                    small = psum_m[1][:, SMALL:SMALL + 2 * E]
                    if s.has(2):
                        pe.wait_ge(ring_read, s.ring("o", 1) + 1)
                        pe.matmul(psum_m[1][:, 0:D], ones_bf[:, :], b_proj_parts[:, :], start=True, stop=False)
                        for c in range(KC):
                            last = pe.matmul(psum_m[1][:, 0:D], o_t[:, c, :], w_proj_sb[:, c, :], start=False, stop=(c == KC - 1))
                        last.then_inc(proj_done, 1)
                    if s.has(0):
                        pe.wait_ge(shifted_done[0], s.item(0) + 1)
                        for n in range(2):
                            transposes(s, f"p{n}", [shifted[0][:, 4 * n + j, :] for j in range(4)])
                    if s.has(1):
                        pe.wait_ge(ring_read, s.ring("p3", 1) + 1)
                        weigh(s.side(1), 1).then_inc(pv_done, 1)
                    if s.has(-1):
                        pe.wait_ge(q_lo, 2 * (s.item(-1) + 1))
                        parts = q_parts[s.side(-1)][:, :, :, :, :].rearrange("p (j h) c s d -> p j (h c s d)", h=2)
                        transposes(s, "q_a", [parts[:, j, :] for j in range(4)])
                        transposes(s, "q_b", [parts[:, j, :] for j in range(4, 8)])
                    if s.has(1):
                        pe.wait_ge(pv_read, s.item(1) + 1)
                        if s.has(4):
                            pe.wait_ge(logits_read, s.item(4) + 1)
                        elif s.has(2):
                            pe.wait_ge(x2_done, s.item(2) + 1)
                        for g in range(H // QUAD):
                            last = pe.transpose(psum_m[1][:, P * g:P * g + P], pv_t[:, g, :], ident)
                        last.then_inc(back_done, 1)
                    if s.has(0):
                        pe.wait_ge(ring_read, s.ring("p1") + 1)
                        pe.wait_ge(v_in[s.side(0)], 16 * (s.turn(0) + 1))
                        weigh(s.side(0), 0)
                    if s.has(3):
                        pe.wait_ge(norm2, s.item(3) + 1)
                        transposes(s, "n", [x2n[:, P * c:P * c + P] for c in range(KC)])
                    if s.has(-1):
                        pe.wait_ge(ring_read, s.ring("q_b") + 1)
                        pe.wait_ge(k_ready, 32 * (s.item(-1) + 1))
                        scores(s, 0)
                    if s.has(0):
                        pe.wait_ge(shifted_done[1], s.item(0) + 1)
                        for n in range(2, 4):
                            transposes(s, f"p{n}", [shifted[1][:, 4 * n - 8 + j, :] for j in range(4)])
                    if s.has(-1):
                        scores(s, 1)
                    if s.has(1):
                        pe.wait_ge(o_done, s.item(1) + 1)
                        flat = o_sb[:, :, :].rearrange("p h d -> p (h d)")
                        transposes(s, "o", [flat[:, P * c:P * c + P] for c in range(KC)])
                    if s.has(4):
                        b = s.item(4)
                        pe.wait_ge(hot_done, b + 1)
                        pe.matmul(small[:, 0:E], before[:, :], hot[s.side(4)][:, :], start=True, stop=False)
                        pe.matmul(small[:, 0:E], ones_bf[:, :], taken[:, :], start=False, stop=True).then_inc(rank_done, 1)
                    if s.has(3):
                        pe.wait_ge(ring_read, s.ring("n") + 1)
                        if s.has(3, 1) and not s.has(1):
                            pe.wait_ge(logits_read, s.item(3))
                        for c in range(KC):
                            last = pe.matmul(small[:, E:2 * E], x2n_t[:, c, :], wr_sb[:, c, :], start=(c == 0), stop=(c == KC - 1))
                        last.then_inc(logits_done, 1)
                walk(pe, FIRST_A, LAST_A, LOOP_A, NB, step)
                pe.wait_ge(taken_done, NB)
                pe.matmul(psum_m[0][:, 0:E], ones_bf[:, :], taken[:, :], start=True, stop=True).then_inc(counted, 1)

            @block.vector
            def _(dve):
                def prepare():
                    dve.memset(k_t[:, :, :, :].bitcast(F32), 0.0).then_inc(consts_set, 1)
                    dve.memset(psum_m[0][:, :], 0.0).then_inc(consts_set, 1)
                    dve.memset(ones_bf[:, :], 1.0).then_inc(consts_set, 1)
                    dve.wait_ge(cst_in, 16)
                    dve.tensor_copy(before[:, :], const("before")).then_inc(consts_set, 1)
                    dve.tensor_copy(taken[:, :], const("taken_first")).then_inc(consts_set, 1)
                    dve.wait_ge(consts_in, CONSTS_IN)
                    split, rest, kept = sem("split"), o_sb[:, :, :].rearrange("p h d -> p (h d)"), xr_sb[1][:, :]
                    dve.tensor_copy(b_proj_parts[:, :], b_proj_sb[:, :]).then_inc(split, 1)
                    dve.wait_ge(split, 1)
                    dve.tensor_tensor(rest, b_proj_sb[:, :], b_proj_parts[:, :], ALU.subtract).then_inc(split, 1)
                    dve.tensor_scalar(kept, b_proj_parts[:, :], const("part0"), None, ALU.mult).then_inc(split, 1)
                    dve.wait_ge(split, 3)
                    dve.tensor_copy(b_proj_parts[:, :], rest).then_inc(split, 1)
                    dve.wait_ge(split, 4)
                    dve.scalar_tensor_tensor(out=kept, in0=b_proj_parts[:, :], scalar=const("part1"), in1=kept,
                                             op0=ALU.mult, op1=ALU.add).then_inc(split, 1)
                    dve.tensor_tensor(rest, rest, b_proj_parts[:, :], ALU.subtract).then_inc(split, 1)
                    dve.wait_ge(split, 6)
                    dve.scalar_tensor_tensor(out=kept, in0=rest, scalar=const("part2"), in1=kept,
                                             op0=ALU.mult, op1=ALU.add).then_inc(split, 1)
                    dve.wait_ge(split, 7)
                    dve.tensor_copy(b_proj_parts[:, :], kept).then_inc(consts_set, 1)

                def largest(s, half):
                    b = s.item(0)
                    dve.wait_ge(scores_done[half], b + 1)
                    dve.tensor_reduce(smax[:, 8 * half:8 * half + 8], psum_s[half][:, :, :], AX.X, ALU.max).then_inc(row_max, 1)

                def shift(s, half):
                    b = s.item(0)
                    dve.wait_ge(row_max, 2 * b + half + 1)
                    dve.tensor_tensor(shifted[half][:, :, :], psum_s[half][:, :, :],
                                      repeat_last(smax[:, 8 * half:8 * half + 8], P), ALU.subtract).then_inc(shifted_done[half], 1)

                def step(s):
                    if s.fixed and s.number == -3:
                        prepare()
                    small = psum_m[1][:, SMALL:SMALL + 2 * E]
                    n0, n1, n2, n4, n5, nw = (s.has(lag) for lag in (0, 1, 2, 4, 5, -4))
                    b1_, b2_, b4, b5, bw = (s.item(lag) for lag in (1, 2, 4, 5, -4))
                    if n0:
                        largest(s, 0)
                    if n0:
                        shift(s, 0)
                    if n0:
                        largest(s, 1)
                    if nw:
                        dve.wait_ge(x_in[s.side(-4, 4)], 16 * (s.turn(-4, 4) + 1))
                        if s.has(-4, 1) and not s.has(0, 1):
                            dve.wait_ge(stats1, CHAIN * bw)
                        dve.bn_stats(st1[:, :], x_sb[s.side(-4, 4)][:, :]).then_inc(stats1, 1)
                    if n2:
                        r2 = s.side(2, 4)
                        dve.wait_ge(proj_done, b2_ + 1)
                        dve.wait_ge(xr_in[s.side(2)], 16 * (s.turn(2) + 1))
                        if s.has(2, 4):
                            dve.wait_ge(row_out[r2], 16 * s.turn(2, 4))
                        dve.tensor_tensor(row[r2][:, 0:D], psum_m[1][:, 0:D], xr_sb[s.side(2)][:, :], ALU.add).then_inc(x2_done, 1)
                    if n4:
                        dve.wait_ge(logits_done, b4 + 1)
                    if n5:
                        h5 = hot[s.side(5)][:, :]
                        dve.wait_ge(rank_done, b5 + 1)
                        if s.has(5, 1) and not n0:
                            dve.wait_ge(place_done, b5)
                        dve.tensor_tensor_reduce(spot_x[:, :], small[:, 0:E], h5, 1.0, 0.0, ALU.mult, ALU.add,
                                                 spot_f[:, :]).then_inc(place, 1)
                    if n4:
                        if s.has(4, 1) and not n0:
                            dve.wait_ge(hot_done, b4)
                        dve.tensor_tensor(logits[:, :], small[:, E:2 * E], b_r_sb[:, :], ALU.add).then_inc(logits_read, 1)
                    if n4:
                        dve.wait_ge(logits_read, b4 + 1)
                    if n5:
                        if not n4:
                            dve.wait_ge(place, b5 + 1)
                        dve.tensor_scalar(spot_i[s.side(5, 4)][:, :], spot_f[:, :], float(E // 2 * REGION), None, ALU.add).then_inc(place_done, 1)
                    if n4:
                        dve.max(top[:, :], logits[:, :]).then_inc(choice, 1)
                    if n2:
                        if not n4:
                            dve.wait_ge(x2_done, b2_ + 1)
                        dve.bn_stats(st2[:, :], row[r2][:, 0:D]).then_inc(stats2, 1)
                    if n4:
                        dve.wait_ge(choice, 3 * b4 + 1)
                    if nw:
                        if not n4:
                            dve.wait_ge(stats1, CHAIN * bw + 1)
                        if s.has(-4, 2):
                            dve.wait_ge(shift1, bw - 1)
                    if n2 and not nw and s.has(2, 2):
                        dve.wait_ge(shift2, b2_ - 1)
                    if n5:
                        dve.tensor_tensor(taken[:, :], taken[:, :], h5, ALU.add).then_inc(taken_done, 1)
                    if n4:
                        dve.max_index(top_at[:, :], top[:, :], logits[:, :]).then_inc(choice, 1)
                    if nw:
                        dve.bn_aggr(mv1[s.side(-4)][:, :], st1[:, :]).then_inc(stats1, 1)
                    if n4:
                        dve.wait_ge(choice, 3 * b4 + 2)
                        dve.tensor_copy(top_f[:, :], top_at[:, 0:1]).then_inc(choice, 1)
                    if n2:
                        if not n4:
                            dve.wait_ge(stats2, CHAIN * b2_ + 1)
                        dve.bn_aggr(mv2[s.side(2)][:, :], st2[:, :]).then_inc(stats2, 1)
                    if n0:
                        shift(s, 1)
                    if n1:
                        sums = psum_m[1][:, :].rearrange("p (h e) -> p h e", h=H)
                        dve.wait_ge(back_done, b1_ + 1)
                        dve.reciprocal(recip[:, :], sums[:, :, DH]).then_inc(recip_done, 1)
                    if n4:
                        dve.wait_ge(choice, 3 * b4 + 3)
                        dve.tensor_scalar(hot[s.side(4)][:, :], const("expert"), top_f[:, 0:1], None, ALU.is_equal).then_inc(hot_done, 1)
                    if n2:
                        dve.wait_ge(stats2, CHAIN * b2_ + 2)
                        dve.tensor_scalar(ve2[s.side(2)][:, :], mv2[s.side(2)][:, 1:2], EPS, None, ALU.add).then_inc(stats2, 1)
                    if nw:
                        if not n2:
                            dve.wait_ge(stats1, CHAIN * bw + 2)
                        dve.tensor_scalar(ve1[s.side(-4)][:, :], mv1[s.side(-4)][:, 1:2], EPS, None, ALU.add).then_inc(stats1, 1)
                    if n1:
                        dve.wait_ge(recip_done, b1_ + 1)
                        dve.tensor_tensor(o_sb[:, :, :], sums[:, :, 0:DH], repeat_last(recip[:, :], DH), ALU.mult).then_inc(o_done, 1)
                walk(dve, FIRST_A, LAST_A, LOOP_A, NB, step)

                at = [0]

                def then(ins):
                    ins.then_inc(plan, 1)
                    at[0] += 1
                    dve.wait_ge(plan, at[0])

                free = [0, 0]

                def table(half, *shape):
                    n = int(np.prod(shape))
                    a, free[half] = free[half], free[half] + n
                    t = shifted[half][:, :, :].rearrange("p j s -> p (j s)")[:, a:a + n]
                    return t if len(shape) == 1 else t.rearrange("p (a b) -> p a b", b=shape[1])
                count, pad_f, tiles_of, tiles_to, tiles_at, region_less = (table(0, E) for _ in range(6))
                over = table(0, E, TOK // P)
                expert_f, row_f, row_g, row_h, row_k = (table(0, TILES) for _ in range(5))
                past, is_expert, row_part = (table(1, TILES, E) for _ in range(3))

                dve.wait_ge(counted, 1)
                then(dve.tensor_tensor(count[:, :], psum_m[0][:, 0:E], const("count_back"), ALU.add))
                then(dve.tensor_tensor(pad_f[:, :], count[:, :], const("region"), ALU.add))
                dve.tensor_copy(pad_row[:, :], pad_f[:, :]).then_inc(pads_placed, 1)
                then(dve.tensor_tensor(over[:, :, :], repeat_last(count[:, :], TOK // P), spread(const("full_rows"), 1, E), ALU.is_gt))
                then(dve.tensor_reduce(tiles_of[:, :], over[:, :, :], AX.X, ALU.add))
                then(dve.tensor_tensor_scan(tiles_to[:, :], tiles_of[:, :], tiles_of[:, :], 0.0, ALU.add, ALU.bypass))
                then(dve.tensor_tensor(tiles_at[:, :], tiles_to[:, :], tiles_of[:, :], ALU.subtract))
                then(dve.scalar_tensor_tensor(out=region_less[:, :], in0=tiles_at[:, :], scalar=-float(P), in1=const("region"),
                                              op0=ALU.mult, op1=ALU.add))
                then(dve.tensor_tensor(past[:, :, :], spread(tiles_to[:, :], 1, TILES), repeat_last(const("tile"), E), ALU.is_le))
                then(dve.tensor_reduce(expert_f[:, :], past[:, :, :], AX.X, ALU.add))
                then(dve.tensor_tensor(is_expert[:, :, :], repeat_last(expert_f[:, :], E), spread(const("expert"), 1, TILES), ALU.is_equal))
                then(dve.tensor_tensor(row_part[:, :, :], is_expert[:, :, :], spread(region_less[:, :], 1, TILES), ALU.mult))
                then(dve.tensor_reduce(row_f[:, :], row_part[:, :, :], AX.X, ALU.add))
                then(dve.tensor_tensor(row_g[:, :], row_f[:, :], const("tile_row"), ALU.add))
                then(dve.tensor_scalar(row_h[:, :], expert_f[:, :], float(E), float(SPARE), ALU.is_ge, ALU.mult))
                then(dve.tensor_tensor(row_k[:, :], row_g[:, :], row_h[:, :], ALU.add))
                dve.tensor_scalar(tile_row[:, :], row_k[:, :], float(SPARE), None, ALU.min).then_inc(tables, 1)
                dve.tensor_scalar(tile_expert[:, :], expert_f[:, :], float(E - 1), None, ALU.min).then_inc(tables, 1)

        with ExitStack() as f:
            b2_sb = sb("b2_sb", [P, E, D], F32, f)
            w_now = [sb(f"w_now{i}", [P, KC, F], F32, f) for i in range(2)]
            b1_now = [sb(f"b1_now{i}", [P, FC], F32, f) for i in range(2)]
            t_in = [sb(f"t_in{i}", [P, ROW], F32, f) for i in range(4)]
            t_res = [sb(f"t_res{i}", [P, D + 1], F32, f) for i in range(2)]
            t_id = [sb(f"t_id{i}", [P, 1], U32, f) for i in range(2)]
            t_n = [sb(f"t_n{i}", [P, D], F32, f) for i in range(2)]
            t_nt = [sb(f"t_nt{i}", [P, KC, P], F32, f) for i in range(2)]
            hid = [sb(f"hid{i}", [P, FC, P], F32, f) for i in range(2)]
            t_out = [sb(f"t_out{i}", [P, D], F32, f) for i in range(2)]
            st = sb("st", [P, 6], F32, f)
            mv = sb("mv", [P, 2], F32, f)
            ve = sb("ve", [P, 1], F32, f)
            rs = sb("rs", [P, 1], F32, f)
            b2_in = sem("b2_in")
            t_loaded, t_done = [sem(f"t_loaded{i}") for i in range(4)], sems("t_done")
            t_root = sem("t_root")
            t_ln, t_kept, t_turned, t_turned_read = sem("t_ln"), sem("t_kept"), sem("t_turned"), sem("t_turned_read")
            w1_set, b1_set = sem("w1_set"), sem("b1_set")
            hid_done, hid_read, y_done, y_read = sem("hid_done"), sem("hid_read"), sem("y_done"), sem("y_read")

            block = f.enter_context(nc.Block())

            @block.sync
            def _(sp):
                sp.wait_ge(pads_out, 16 * E)
                sp.wait_ge(tables, 2)

                def step(s):
                    if s.has(-3):
                        p = s.side(-3, 4)
                        row = sp.value_load(tile_row[0:1, bass.ds(s.item(-3), 1)], min_val=0, max_val=SPARE)
                        if s.has(-3, 4):
                            sp.wait_ge(t_kept, 2 * (s.item(-3) - 3))
                        sp.dma_start(t_in[p][:, :], routed[bass.ds(row, P), :]).then_inc(t_loaded[p], 16)
                        if s.fixed and s.item(-3) == 1:
                            sp.dma_start(b2_sb[:, :, :].rearrange("p e d -> p (e d)"), spread(b2, 0, P)).then_inc(b2_in, 16)
                walk(sp, FIRST_F, LAST_F, LOOP_F, TILES, step)

            @block.gpsimd
            def _(pool):
                def step(s):
                    if s.has(2):
                        pool.wait_ge(y_read, 2 * (s.item(2) + 1))
                    if s.has(-2):
                        pool.wait_ge(t_ln, (CHAIN + 1) * s.item(-2) + CHAIN)
                        pool.tensor_tensor(rs[:, :], ve[:, :], const("power"), ALU.pow).then_inc(t_root, 1)
                    if s.has(2):
                        p = s.side(2)
                        pool.indirect_dma_start(
                            out=out_rows, out_offset=bass.IndirectOffsetOnAxis(ap=t_id[p][:, 0:1], axis=0),
                            in_=t_out[p][:, :], in_offset=None, bounds_check=TOK - 1, oob_is_err=False).then_inc(t_done[p], 16)
                walk(pool, FIRST_F, LAST_F, LOOP_F, TILES, step)
                for p in range(2):
                    pool.wait_ge(t_done[p], 16 * ((TILES + 1 - p) // 2))

            @block.scalar
            def _(act):
                def step(s):
                    if s.has(-1):
                        p = s.side(-1)
                        act.wait_ge(t_turned, s.item(-1) + 1)
                        if s.has(-1, 2):
                            act.wait_ge(hid_done, 2 * (s.item(-1) - 1))
                        act.activation(t_nt[p][:, :, :], psum_r[p][:, 0:D].rearrange("p (c t) -> p c t", c=KC), ACT.Copy).then_inc(t_turned_read, 1)
                    if s.has(0):
                        p = s.side(0)
                        act.wait_ge(b1_set, s.item(0) + 1)
                        if s.has(0, 2):
                            act.wait_ge(y_done, s.item(0) - 1)
                        for c in range(FC):
                            if c % 4 == 0:
                                act.wait_ge(hid_done, 2 * s.item(0) + c // 4 + 1)
                            act.activation(hid[p][:, c, :], psum_s[p][:, c, :], ACT.Relu, bias=b1_now[p][:, c:c + 1]).then_inc(hid_read, 1)
                walk(act, FIRST_F, LAST_F, LOOP_F, TILES, step)

            @block.tensor
            def _(pe):
                pe.wait_ge(tables, 2)
                pe.wait_ge(experts_in, 16 * NB)

                def turn_next(s):
                    b, p = s.item(-1), s.side(-1)
                    pe.wait_ge(t_ln, (CHAIN + 1) * (b + 1))
                    if s.has(-1, 2):
                        pe.wait_ge(t_turned_read, b - 1)
                    for c in range(KC):
                        last = pe.transpose(psum_r[p][:, P * c:P * c + P], t_n[p][:, P * c:P * c + P], ident)
                    last.then_inc(t_turned, 1)

                def step(s):
                    if s.has(-1) and (s.has(1) or not s.has(0)):
                        turn_next(s)
                    if s.has(1):
                        b, p = s.item(1), s.side(1)
                        e = pe.value_load(tile_expert[0:1, bass.ds(b, 1)], min_val=0, max_val=E - 1)
                        if s.has(1, 2):
                            pe.wait_ge(y_read, 2 * (b - 1))
                        for c in range(FC):
                            if c % 4 == 0:
                                pe.wait_ge(hid_read, FC * b + c + 4)
                            w2 = w_sb[:, bass.ds(4 * e + 2 + c // 4, 1), D * (c % 4):D * (c % 4 + 1)].rearrange("p a d -> p (a d)")
                            last = pe.matmul(psum_m[p][:, 0:D], hid[p][:, c, :], w2, start=(c == 0), stop=(c == FC - 1))
                        last.then_inc(y_done, 1)
                    if s.has(0):
                        b, p = s.item(0), s.side(0)
                        pe.wait_ge(t_turned_read, b + 1)
                        pe.wait_ge(w1_set, b + 1)
                        if s.has(0, 2):
                            pe.wait_ge(hid_read, FC * (b - 1))
                        for c in range(FC):
                            for k in range(KC):
                                last = pe.matmul(psum_s[p][:, c, :], w_now[p][:, k, P * c:P * c + P], t_nt[p][:, k, :],
                                                 start=(k == 0), stop=(k == KC - 1))
                            if c % 4 == 3:
                                last.then_inc(hid_done, 1)
                    if s.has(-1) and s.has(0) and not s.has(1):
                        turn_next(s)
                walk(pe, FIRST_F, LAST_F, LOOP_F, TILES, step)

            @block.vector
            def _(dve):
                dve.wait_ge(tables, 2)
                dve.wait_ge(experts_in, 16 * NB)

                def first_layer(s):
                    q = s.side(-1)
                    e = dve.value_load(tile_expert[0:1, bass.ds(s.item(-1), 1)], min_val=0, max_val=E - 1)
                    if s.has(-1, 2):
                        dve.wait_ge(hid_done, 2 * (s.item(-1) - 1))
                    dve.tensor_copy(w_now[q][:, :, :], w_sb[:, bass.ds(4 * e, 2), :]).then_inc(w1_set, 1)
                    return e

                ahead = first_layer(Step(-1, UNROLL - 1, TILES))

                def step(s):
                    if s.has(-2):
                        b, p, p4 = s.item(-2), s.side(-2), s.side(-2, 4)
                        base = (CHAIN + 1) * b
                        dve.wait_ge(t_loaded[p4], 16 * (s.turn(-2, 4) + 1))
                        if s.has(-2, 1):
                            dve.wait_ge(t_ln, base)
                        dve.bn_stats(st[:, :], t_in[p4][:, 0:D]).then_inc(t_ln, 1)
                        dve.wait_ge(t_ln, base + 1)
                    if s.has(-1):
                        e = ahead if s.fixed and s.item(-1) == 0 else first_layer(s)
                    if s.has(-2):
                        dve.bn_aggr(mv[:, :], st[:, :]).then_inc(t_ln, 1)
                        dve.wait_ge(t_ln, base + 2)
                        dve.tensor_scalar(ve[:, :], mv[:, 1:2], EPS, None, ALU.add).then_inc(t_ln, 1)
                    if s.has(0):
                        r, r4 = s.side(0), s.side(0, 4)
                        e0 = dve.value_load(tile_expert[0:1, bass.ds(s.item(0), 1)], min_val=0, max_val=E - 1)
                        if s.has(0, 2):
                            dve.wait_ge(y_read, 2 * (s.item(0) - 1))
                        elif s.item(0) == 0:
                            dve.wait_ge(b2_in, 16)
                        dve.tensor_tensor(t_res[r][:, 0:D], t_in[r4][:, 0:D], b2_sb[:, bass.ds(e0, 1), :].rearrange("p a d -> p (a d)"),
                                          ALU.add).then_inc(t_kept, 1)
                        dve.tensor_copy(t_res[r][:, D:D + 1], t_in[r4][:, D:D + 1]).then_inc(t_kept, 1)
                    if s.has(-2):
                        dve.wait_ge(t_root, b + 1)
                        if s.has(-2, 2):
                            dve.wait_ge(t_turned, b - 1)
                        dve.tensor_scalar(t_n[p][:, :], t_in[p4][:, 0:D], mv[:, 0:1], rs[:, 0:1], ALU.subtract, ALU.mult).then_inc(t_ln, 1)
                    if s.has(1):
                        q = s.side(1)
                        dve.wait_ge(y_done, s.item(1) + 1)
                        if s.has(1, 2):
                            dve.wait_ge(t_done[q], 16 * s.turn(1))
                        dve.wait_ge(t_kept, 2 * (s.item(1) + 1))
                        dve.tensor_tensor(t_out[q][:, :], psum_m[q][:, 0:D], t_res[q][:, 0:D], ALU.add).then_inc(y_read, 1)
                        dve.tensor_copy(t_id[q][:, :], t_res[q][:, D:D + 1]).then_inc(y_read, 1)
                    if s.has(-1):
                        if s.has(-1, 2):
                            dve.wait_ge(hid_read, FC * (s.item(-1) - 1))
                        dve.tensor_copy(b1_now[s.side(-1)][:, :], b1_sb[:, bass.ds(e, 1), :].rearrange("p a c -> p (a c)")).then_inc(b1_set, 1)
                walk(dve, FIRST_F, LAST_F, LOOP_F, TILES, step)


def constants():
    t = np.zeros((P, CONST_WIDTH), np.float32)

    def put(name, value):
        a, b = CONST_COLS[name]
        t[:, a:b] = value
    lane = np.arange(P)
    put("ident", np.eye(P))
    put("before", lane[:, None] < lane[None, :])
    put("region", REGION * np.arange(E)[None])
    put("taken_first", REGION // P * (np.arange(E)[None] - E // 2))
    put("count_back", REGION * (E // 2 - np.arange(E)[None]))
    put("expert", np.arange(E)[None])
    put("full_rows", P * np.arange(TOK // P)[None])
    put("tile", np.arange(TILES)[None])
    put("tile_row", P * np.arange(TILES)[None])
    put("minus_hi", -(lane // 32 % 2)[:, None])
    put("lane", lane[:, None])
    put("power", -0.5)
    put("round", UNROLL * P)
    for part in range(3):
        put(f"part{part}", (lane == part)[:, None])
    return t


def kernel(x, ctx_1024, L0_xattn_w_proj, L0_xattn_b_proj, L0_ffn_Wr, L0_ffn_br, L0_ffn_W1, L0_ffn_b1, L0_ffn_W2, L0_ffn_b2):
    import concourse.bacc as bacc
    from concourse.bass_utils import run_bass_kernel_spmd

    x = np.asarray(x)
    ctx = np.asarray(ctx_1024)
    heads = ctx.reshape(NB, P, PAIRS, 2, DH).transpose(0, 3, 4, 2, 1)
    w1 = np.asarray(L0_ffn_W1).transpose(0, 2, 1).reshape(E, 2, P, F)
    w2 = np.asarray(L0_ffn_W2).transpose(0, 2, 1).reshape(E, 2, FC // 2, P, D).transpose(0, 1, 3, 2, 4).reshape(E, 2, P, F)
    arrays = {
        "x": x,
        "ctx_rows": np.concatenate([ctx.reshape(TOK, H, DH), np.ones((TOK, H, 1), ctx.dtype)], axis=2).reshape(TOK, H * (DH + 1)),
        "ctx_heads": heads,
        "w_proj_t": np.asarray(L0_xattn_w_proj).T,
        "b_proj": np.asarray(L0_xattn_b_proj).reshape(1, D),
        "wr_t": np.asarray(L0_ffn_Wr).T,
        "b_r": np.asarray(L0_ffn_br).reshape(1, E),
        "experts": np.concatenate([w1, w2], axis=1).reshape(4 * E, P, F),
        "b1_cols": np.asarray(L0_ffn_b1).reshape(E, FC, P).transpose(2, 0, 1),
        "b2": np.asarray(L0_ffn_b2).reshape(1, E * D),
        "consts": constants(),
    }
    arrays = {f"in_{k}": np.ascontiguousarray(v) for k, v in arrays.items()}
    nc = bacc.Bacc("TRN2", target_bir_lowering=False, num_devices=1)
    args = [nc.dram_tensor(k, v.shape, mybir.dt.from_np(v.dtype), kind="ExternalInput").ap() for k, v in arrays.items()]
    out = nc.dram_tensor("out", (NB, P, D), F32, kind="ExternalOutput").ap()
    build(nc, *args, out)
    r = run_bass_kernel_spmd(nc, [arrays], core_ids=[0])
    return r.results[0]["out"]
```
